# Optimizing a Trainium2 kernel written in Bass

```python
import numpy as np
import jax
import jax.numpy as jnp

def _softmax(x, axis=-1):
    return jax.nn.softmax(x, axis=axis)

def _gelu(x):
    return jax.nn.gelu(x, approximate=True)

def _silu(x):
    return jax.nn.silu(x)

def _sigmoid(x):
    return jax.nn.sigmoid(x)

def _layernorm(x, axis=-1, eps=1e-05):
    m = jnp.mean(x, axis=axis, keepdims=True)
    v = jnp.var(x, axis=axis, keepdims=True)
    return (x - m) / jnp.sqrt(v + eps)

def _scatter_add(tgt, idx, src, axis=0):
    return tgt.at[idx].add(src)

def _segment_sum(src, seg, n):
    return jax.ops.segment_sum(src, seg, n)
kernel_name = 'mk_gnn_preln_d1_gnn_r8_7c8c53'

def setup_inputs(seed: int=0):
    np.random.seed(seed)
    _w = jnp.asarray

    def _rec_inputs():
        import jax
        import jax.numpy as jnp
        _gk = jax.random.key(seed)
        x = -0.0005121 + 1.001 * jax.random.normal(jax.random.fold_in(_gk, 1), (6250, 64), jnp.float32)
        src = jax.random.randint(jax.random.fold_in(_gk, 2), (200000,), 0, 6250, jnp.int32)
        dst = jnp.minimum((6250 * jax.random.uniform(jax.random.fold_in(_gk, 3), (200000,)) ** 2.0).astype(jnp.int32), 49999)
        _o = jnp.argsort(dst, stable=True)
        src = src[_o]
        dst = dst[_o]
        edge_attr_64 = 0.000189758 + 1.00013 * jax.random.normal(jax.random.fold_in(_gk, 12), (200000, 64), jnp.float32)
        return (x, src, dst, edge_attr_64)
    x, src, dst, edge_attr_64 = _rec_inputs()

    def _L0_gnn_setup():
        import jax, jax.numpy as jnp
        import numpy as np
        N_NODES = 6250
        N_EDGES = 100000
        D_NODE = 64
        HID = 64
        N_TGT = 64

        def _init_linear(key, fan_in, fan_out):
            kw, kb = jax.random.split(key)
            bound = 1.0 / np.sqrt(fan_in)
            W = jax.random.uniform(kw, (fan_in, fan_out), minval=-bound, maxval=bound, dtype=jnp.float32)
            b = jax.random.uniform(kb, (fan_out,), minval=-bound, maxval=bound, dtype=jnp.float32)
            return (W, b)
        key = jax.random.key(seed)
        ks = jax.random.split(key, 8)
        x = jax.random.normal(ks[0], (N_NODES, D_NODE), dtype=jnp.float32)
        edge_index = jax.random.randint(ks[1], (2, N_EDGES), 0, N_NODES, dtype=jnp.int64)
        edge_attr = jax.random.normal(ks[2], (N_EDGES, HID), dtype=jnp.float32)
        u = jax.random.normal(ks[3], (1, 16), dtype=jnp.float32)
        batch = jnp.zeros((N_NODES,), dtype=jnp.int64)
        W1a, b1a = _init_linear(ks[4], D_NODE + HID, HID)
        W1b, b1b = _init_linear(ks[5], HID, HID)
        W2a, b2a = _init_linear(ks[6], D_NODE + HID, HID)
        W2b, b2b = _init_linear(ks[7], HID, N_TGT)
        return {'x': x, 'edge_index': edge_index, 'edge_attr': edge_attr, 'u': u, 'batch': batch, 'W1a': W1a, 'b1a': b1a, 'W1b': W1b, 'b1b': b1b, 'W2a': W2a, 'b2a': b2a, 'W2b': W2b, 'b2b': b2b}
    _L0_gnn_all = _L0_gnn_setup()
    _L0_gnn_in = {k: v for k, v in _L0_gnn_all.items() if k in ('u', 'W1a', 'b1a', 'W1b', 'b1b', 'W2a', 'b2a', 'W2b', 'b2b')}
    del _L0_gnn_all
    return {'x': x, 'src': src, 'dst': dst, 'edge_attr_64': edge_attr_64, 'L0_gnn_u': _L0_gnn_in['u'], 'L0_gnn_W1a': _L0_gnn_in['W1a'], 'L0_gnn_b1a': _L0_gnn_in['b1a'], 'L0_gnn_W1b': _L0_gnn_in['W1b'], 'L0_gnn_b1b': _L0_gnn_in['b1b'], 'L0_gnn_W2a': _L0_gnn_in['W2a'], 'L0_gnn_b2a': _L0_gnn_in['b2a'], 'L0_gnn_W2b': _L0_gnn_in['W2b'], 'L0_gnn_b2b': _L0_gnn_in['b2b']}

def reference(x, src, dst, edge_attr_64, L0_gnn_u, L0_gnn_W1a, L0_gnn_b1a, L0_gnn_W1b, L0_gnn_b1b, L0_gnn_W2a, L0_gnn_b2a, L0_gnn_W2b, L0_gnn_b2b):
    import jax
    import jax.numpy as jnp

    def _L0_gnn_ref(x, edge_index, edge_attr, u, batch, W1a, b1a, W1b, b1b, W2a, b2a, W2b, b2b):
        import jax, jax.numpy as jnp
        import numpy as np
        N_NODES = 6250
        N_EDGES = 100000
        D_NODE = 64
        HID = 64
        N_TGT = 64

        def _init_linear(key, fan_in, fan_out):
            kw, kb = jax.random.split(key)
            bound = 1.0 / np.sqrt(fan_in)
            W = jax.random.uniform(kw, (fan_in, fan_out), minval=-bound, maxval=bound, dtype=jnp.float32)
            b = jax.random.uniform(kb, (fan_out,), minval=-bound, maxval=bound, dtype=jnp.float32)
            return (W, b)
        row, col = (edge_index[0], edge_index[1])
        msg = jnp.concatenate([x[col], edge_attr], axis=1)
        msg = jnp.maximum(msg @ W1a + b1a, 0.0) @ W1b + b1b
        summed = jax.ops.segment_sum(msg, row, num_segments=x.shape[0])
        counts = jax.ops.segment_sum(jnp.ones((row.shape[0],), msg.dtype), row, num_segments=x.shape[0])
        agg = summed / jnp.maximum(counts, 1.0)[:, None]
        h = jnp.concatenate([x, agg], axis=1)
        out = jnp.maximum(h @ W2a + b2a, 0.0) @ W2b + b2b
        return out
    edge_index = jnp.stack([src, dst])
    batch0 = jnp.zeros((6250,), jnp.int32)
    h = jnp.maximum(_layernorm(x, axis=-1), 0.0)
    x = x + _L0_gnn_ref(h, edge_index, edge_attr_64, L0_gnn_u, batch0, L0_gnn_W1a, L0_gnn_b1a, L0_gnn_W1b, L0_gnn_b1b, L0_gnn_W2a, L0_gnn_b2a, L0_gnn_W2b, L0_gnn_b2b)
    return x

_drawn_inputs = setup_inputs


def setup_inputs(seed=0):
    import zlib

    import numpy as np

    out = dict(_drawn_inputs(seed))
    spreads = {}
    factors = {'edge_attr_64': 8.0,
     'L0_gnn_W1a': 6.748,
     'L0_gnn_b1a': 8.0,
     'L0_gnn_W1b': 2.915,
     'L0_gnn_b1b': 5.064,
     'L0_gnn_b2a': 5.473}
    for name, (base, spread) in spreads.items():
        noise = np.random.default_rng([zlib.crc32(name.encode()), seed]).standard_normal(out[name].shape)
        drawn = base * np.exp(spread * noise) if base else spread * noise
        out[name] = jnp.asarray(drawn.astype(out[name].dtype))
    for name, factor in factors.items():
        out[name] = (out[name] * factor).astype(out[name].dtype)
    return out
```

```python
import concourse.bass as bass
from concourse import mybir
from contextlib import ExitStack

N_NODES, D, N_EDGES = 6250, 64, 200000
P = 128
TPG = 4
GE = P * TPG
RING = 4
TURNS = -(-N_EDGES // (GE * RING))
GROUPS = TURNS * RING
EXTRA = 8
ALL = GROUPS + EXTRA
EDGES = ALL * GE
COLS = EDGES // P
ROWP = ALL // RING
NT = -(-N_NODES // P)
NT += -NT % TPG
NTURNS = NT // TPG
NODES = NT * P
W = D + 1
PAD_NODE = N_NODES
TRASH = N_NODES + 1
REUSE = 1
TABLES = TPG * REUSE
WIN = P - D
START = RING + 1
EPS = 1e-5

C_W1A_TOP = 0
C_W1A_BOT = C_W1A_TOP + D
C_W1B_T = C_W1A_BOT + RING * D
C_W2A_TOP = C_W1B_T + W
C_W2A_BOT = C_W2A_TOP + D
C_W2B = C_W2A_BOT + D
WCOLS = C_W2B + D


def done(n):
    return n + START


def gnn_kernel(nc, x, e_t, src_col, dst_col, src_row, dst_row, weights, out):
    f32, i32, bf16 = mybir.dt.float32, mybir.dt.int32, mybir.dt.bfloat16
    ALU, ACT, AX = mybir.AluOpType, mybir.ActivationFunctionType, mybir.AxisListType
    assert TRASH + P <= NODES

    with ExitStack() as ctx:
        def sb(name, shape, dt=f32):
            return ctx.enter_context(nc.sbuf_tensor(name, shape, dt))

        def pb(name, shape, dt=f32):
            return ctx.enter_context(nc.psum_tensor(name, shape, dt))

        def sem(name):
            return ctx.enter_context(nc.semaphore(name))

        p_table = nc.dram_tensor("p_table", [NODES, D], f32).ap()
        digits = nc.dram_tensor("digits", [4, EDGES], bf16).ap()
        bases = nc.dram_tensor("bases", [1, ALL], i32).ap()
        sums = [nc.dram_tensor(f"sums{k}", [NODES, W], f32).ap() for k in range(TABLES)]

        ident = sb("ident", [P, P])
        upto = sb("upto", [P, P])
        spread = sb("spread", [4, 2, P], bf16)
        wts = sb("wts", [P, WCOLS])
        wc = sb("wc", [W, D])
        trash_i = sb("trash_i", [P, 1], i32)
        trash = sb("trash", [P, 1])
        epsb = sb("epsb", [P, 1])
        ones = sb("ones", [ROWP, P])

        xs = sb("xs", [P, NT, D])
        xc = sb("xc", [P, NT, D])
        stat = sb("stat", [P, 3, NT])
        h_st = sb("h_st", [P, 2, TPG, D])
        ht_st = sb("ht_st", [W, 2, GE])
        ht = sb("ht", [W, NODES])
        tab = [sb(f"tab{k}", [P, NT * W]) for k in range(4)]
        a_st = sb("a_st", [P, 2, TPG, W])
        at_st = sb("at_st", [W, 2, GE])
        hid_st = sb("hid_st", [W, 2, GE])
        sq = tab[1][:, 0:NT * D].rearrange("p (t d) -> p t d", d=D)

        srcf = sb("srcf", [P, COLS])
        src_t = sb("src_t", [P, COLS])
        dsti = sb("dsti", [P, COLS], i32)
        basew = sb("basew", [P, ALL])
        base_i = sb("base_i", [P, ALL], i32)
        wlane_i = sb("wlane_i", [P, 1], i32)
        wlane = sb("wlane", [P, 1])
        glow = sb("glow", [ROWP, 2, RING])
        glow_i = sb("glow_i", [ROWP, RING], i32)
        wide = sb("wide", [ROWP, RING])
        wides = sb("wides", [ROWP, 1])
        fits = sb("fits", [P, 1])
        fits_i = sb("fits_i", [P, 1], i32)
        ids_i = src_t[:].bitcast(i32)
        row_i = [sb(f"row_i{r}", [ROWP, RING * GE], i32) for r in range(2)]
        dig_i = tab[3][0:ROWP, 0:RING * GE].bitcast(i32)
        dig_j = tab[2][0:ROWP, 0:RING * GE].bitcast(i32)
        dig_b = sb("dig_b", [ROWP, 4, RING * GE], bf16)
        dstf = tab[1][0:ROWP, 0:RING * GE]

        et = sb("et", [P, RING, GE])
        wp = sb("wp", [P, RING, D])
        dig = sb("dig", [4, RING, GE], bf16)
        gidx = sb("gidx", [P, RING, TPG], i32)
        grow = sb("grow", [P, RING, TPG, D])
        same = sb("same", [P, 2, TPG, P])
        rank = sb("rank", [P, 2, TPG])
        pick = sb("pick", [P, 2, TPG])
        sidx = sb("sidx", [P, RING, TPG], i32)
        rr = sb("rr", [P, 2, TPG, W])
        vv = sb("vv", [P, RING, TPG, W])

        srcs_ps = [pb(f"srcs_ps{b}", [P, 512]) for b in range(2)]
        dsts_ps = [pb(f"dsts_ps{b}", [P, 512]) for b in range(2)]
        z_ps = [pb(f"z_ps{b}", [P, 512]) for b in range(2)]
        c_ps = [pb(f"c_ps{b}", [P, 512]) for b in range(2)]

        (x_in, w_in, src_in, dst_in, rows_in0, rows_in1, digits_out, bases_out, base_in, base_row_in, ptab_out,
         res_out) = (
            sem(n) for n in ("x_in", "w_in", "src_in", "dst_in", "rows_in0", "rows_in1", "digits_out", "bases_out",
                             "base_in", "base_row_in", "ptab_out", "res_out"))
        sums_in = [sem(f"sums_in{k}") for k in range(TABLES)]
        rows_in = [rows_in0, rows_in1]
        zeros_ready, consts_ready, ones_ready, digits_ready, bases_ready, wides_ready, fits_raw, flag_ready, wc_raw, wc_ready = (
            sem(n) for n in ("zeros_ready", "consts_ready", "ones_ready", "digits_ready", "bases_ready", "wides_ready",
                             "fits_raw", "flag_ready", "wc_raw", "wc_ready"))
        dve_step, var_ready, std_ready, pool_past, pe_past = (
            sem(n) for n in ("dve_step", "var_ready", "std_ready", "pool_past", "pe_past"))
        h_ready, ht_raw, ht_ready, ht_kept, p_raw, p_ready = (
            sem(n) for n in ("h_ready", "ht_raw", "ht_ready", "ht_kept", "p_raw", "p_ready"))
        et_in, wp_in, dig_in, gathered = ([sem(f"{n}{s}") for s in range(RING)] for n in ("et_in", "wp_in", "dig_in", "gathered"))
        scattered = [sem(f"scattered{k}") for k in range(TABLES)]
        ids_ready, onehot_ready, same_ready, z_ready, zsum_ready, gidx_ready, relu_ready, comb_ready, rows_ready, groups_ended, rank_ready = (
            sem(n) for n in ("ids_ready", "onehot_ready", "same_ready", "z_ready", "zsum_ready", "gidx_ready", "relu_ready",
                             "comb_ready", "rows_ready", "groups_ended", "rank_ready"))
        total_ready, a_ready, at_raw, at_ready, hid_raw, hid_ready, res_raw, res_ready = (
            sem(n) for n in ("total_ready", "a_ready", "at_raw", "at_ready", "hid_raw", "hid_ready", "res_raw", "res_ready"))

        def turns_of_two(eng, turn):
            with eng.Fori(0, NTURNS // 2) as i:
                for b in range(2):
                    turn(b, i * 2 + b)
            if NTURNS % 2:
                turn(0, NTURNS - 1)

        with nc.Block() as block:

            @block.sync
            def _(sp):
                sp.dma_start(xs[:], x.rearrange("(p t) d -> p t d", t=NT)).then_inc(x_in, 16)
                for r, row in enumerate((dst_row, src_row)):
                    sp.dma_start(row_i[r][:], row).then_inc(rows_in[r], 16)
                sp.dma_start(wts[:], weights).then_inc(w_in, 16)
                sp.dma_start(dsti[:], dst_col).then_inc(dst_in, 16)
                for s in range(RING):
                    sp.dma_start(et[0:D, s, :], e_t[:, s * GE:(s + 1) * GE]).then_inc(et_in[s], 16)
                sp.wait_ge(bases_ready, 1)
                sp.dma_start(bases.rearrange("a (p r) -> (a p) r", r=RING), glow_i[:]).then_inc(bases_out, 16)
                sp.wait_ge(digits_ready, 2)
                sp.dma_start(digits[2:4].rearrange("r (p c) -> p r c", p=ROWP), dig_b[:, 2:4, :]).then_inc(digits_out, 16)
                sp.wait_ge(digits_ready, 4)
                sp.dma_start(digits[0:2].rearrange("r (p c) -> p r c", p=ROWP), dig_b[:, 0:2, :]).then_inc(digits_out, 16)
                sp.wait_ge(bases_out, 16)
                sp.dma_start(base_i[:], bases.to_broadcast([P, ALL])).then_inc(base_in, 16)
                sp.wait_ge(base_in, 16)
                sp.wait_ge(digits_out, 32)

                def load(slot, g):
                    base = sp.value_load(base_i[0:1, bass.ds(g, 1)], min_val=0, max_val=N_NODES - 1)
                    sp.dma_start(dig[:, slot, :], digits[:, bass.ds(g * GE, GE)]).then_inc(dig_in[slot], 16)
                    sp.dma_start(wp[D:P, slot, :], p_table[bass.ds(base, WIN), :]).then_inc(wp_in[slot], 16)

                sp.wait_ge(ptab_out, 16)
                for s in range(RING):
                    load(s, s)
                with sp.Fori(0, TURNS) as i:
                    for s in range(RING):
                        g = i * RING + s
                        sp.wait_ge(z_ready, done(g + 1))
                        load(s, g + RING)
                        sp.dma_start(et[0:D, s, :], e_t[:, bass.ds((g + RING) * GE, GE)]).then_inc(et_in[s], 16)
                for s in range(RING):
                    for ring in (et_in, wp_in, dig_in):
                        sp.wait_ge(ring[s], 16 * (TURNS + 1))
                for k in range(TABLES):
                    sp.wait_ge(scattered[k], 16 * (GROUPS // REUSE + 1))
                    sp.dma_start(tab[k][:], sums[k].rearrange("(p t) w -> p (t w)", t=NT)).then_inc(sums_in[k], 16)
                sp.wait_ge(res_ready, done(NTURNS))
                full = N_NODES // NT
                rest = N_NODES - full * NT
                sp.dma_start(out[0:full * NT, :].rearrange("(p t) d -> p t d", t=NT), xc[0:full, :, :]).then_inc(res_out, 16)
                sp.dma_start(out[full * NT:, :].rearrange("(p t) d -> p t d", t=rest),
                             xc[full:full + 1, 0:rest, :]).then_inc(res_out, 16)
                sp.wait_ge(res_out, 32)

            @block.gpsimd
            def _(pool):
                nc.gpsimd.memset(ident[:], 0.0).then_inc(consts_ready, 1)
                nc.gpsimd.memset(upto[:], 1.0).then_inc(consts_ready, 1)
                nc.gpsimd.iota(trash_i[:], pattern=[[0, 1]], base=TRASH, channel_multiplier=1).then_inc(consts_ready, 1)
                nc.gpsimd.iota(wlane_i[:], pattern=[[0, 1]], base=1 - D, channel_multiplier=1).then_inc(consts_ready, 1)
                nc.gpsimd.memset(spread[:], 0.0).then_inc(consts_ready, 1)
                pool.wait_ge(consts_ready, 5)
                nc.gpsimd.affine_select(out=ident[:], in_=ident[:], compare_op=ALU.not_equal, fill=1.0, base=0,
                                        pattern=[[-1, P]], channel_multiplier=1).then_inc(consts_ready, 1)
                nc.gpsimd.affine_select(out=upto[:], in_=upto[:], compare_op=ALU.is_ge, fill=0.0, base=0,
                                        pattern=[[-1, P]], channel_multiplier=1).then_inc(consts_ready, 1)
                nc.gpsimd.affine_select(out=spread[:], in_=spread[:], compare_op=ALU.not_equal, fill=float(P), base=0,
                                        pattern=[[-2, 2], [0, P]], channel_multiplier=1).then_inc(consts_ready, 1)
                pool.wait_ge(consts_ready, 8)
                nc.gpsimd.affine_select(out=spread[:], in_=spread[:], compare_op=ALU.not_equal, fill=1.0, base=-1,
                                        pattern=[[-2, 2], [0, P]], channel_multiplier=1).then_inc(consts_ready, 1)
                nc.gpsimd.memset(tab[0][:], 0.0).then_inc(zeros_ready, 1)
                pool.wait_ge(zeros_ready, 1)
                for k in range(TABLES):
                    pool.dma_start(sums[k].rearrange("(p t) w -> p (t w)", t=NT), tab[0][:]).then_inc(scattered[k], 16)
                pool.sem_inc(ht_kept, START)

                def keep(b, m):
                    pool.wait_ge(ht_ready, done(m + 1))
                    nc.gpsimd.tensor_copy(ht[:, bass.ds(m * GE, GE)], ht_st[:, b, :]).then_inc(ht_kept, 1)

                pool.wait_ge(ones_ready, 5)
                turns_of_two(pool, keep)

                def gather(slot):
                    for k in range(TPG):
                        nc.gpsimd.indirect_dma_start(
                            out=grow[:, slot, k, :], out_offset=None, in_=p_table[:, :],
                            in_offset=bass.IndirectOffsetOnAxis(ap=gidx[:, slot, k:k + 1], axis=0),
                        ).then_inc(gathered[slot], 16)

                def scatter(slot, turn, g):
                    for k in range(TPG):
                        t = (slot % REUSE) * TPG + k
                        if k == 0:
                            pool.wait_ge(same_ready, done(g + 1))
                            pool.wait_ge(rows_ready, done(g + 1))
                        pool.wait_ge(scattered[t], (turn * (RING // REUSE) + slot // REUSE + 1) * 16)
                        pool.sem_inc(pool_past, 1)
                        nc.gpsimd.indirect_dma_start(
                            out=sums[t][:, :],
                            out_offset=bass.IndirectOffsetOnAxis(ap=sidx[:, slot, k:k + 1], axis=0),
                            in_=vv[:, slot, k, :], in_offset=None, compute_op=ALU.add,
                        ).then_inc(scattered[t], 16)
                    pool.sem_inc(groups_ended, 1)

                pool.sem_inc(groups_ended, START - REUSE)
                pool.wait_ge(flag_ready, 1)
                fit = pool.value_load(fits_i[0:1, 0:1], min_val=0, max_val=1)
                with pool.If(fit == 1):
                    with pool.Fori(0, TURNS) as i:
                        for s in range(RING):
                            scatter(s, i, i * RING + s)
                with pool.Else():
                    pool.wait_ge(ptab_out, 16)
                    pool.wait_ge(gidx_ready, done(0))
                    for s in range(RING - 1):
                        gather(s)
                    with pool.Fori(0, TURNS) as i:
                        for s in range(RING):
                            g = i * RING + s
                            pool.wait_ge(gidx_ready, done(g))
                            pool.wait_ge(zsum_ready, done(g))
                            pool.sem_inc(pool_past, 1)
                            gather((s + RING - 1) % RING)
                            scatter(s, i, g)
                    for s in range(RING - 1):
                        pool.wait_ge(gathered[s], 16 * TPG * (TURNS + 1))
                    pool.wait_ge(gathered[RING - 1], 16 * TPG * TURNS)

            @block.scalar
            def _(act):
                act.dma_start(ids_i, src_col).then_inc(src_in, 16)
                act.sem_inc(ht_ready, START)
                act.sem_inc(p_ready, START)
                act.sem_inc(relu_ready, START)
                act.sem_inc(rows_ready, START)
                act.sem_inc(at_ready, START)
                act.sem_inc(hid_ready, START)
                act.wait_ge(w_in, 16)
                act.wait_ge(ones_ready, 1)
                act.wait_ge(var_ready, 1)
                nc.scalar.activation(stat[:, 2, :], stat[:, 1, :], ACT.Sqrt, bias=epsb[:], scale=1.0 / D).then_inc(std_ready, 1)

                def p_rows(b, m):
                    act.wait_ge(ht_raw, done(m + 1))
                    act.wait_ge(ht_kept, done(m - 1))
                    act.wait_ge(p_raw, done(m - 1))
                    nc.scalar.activation(ht_st[0:D, b, :], srcs_ps[b][0:D, :], ACT.Relu).then_inc(ht_ready, 1)

                def p_keep(b, m):
                    act.wait_ge(p_raw, done(m + 1))
                    nc.scalar.activation(xc[:, bass.ds(m * TPG, TPG), :],
                                         z_ps[b][:, 0:TPG * D].rearrange("p (t d) -> p t d", d=D), ACT.Copy).then_inc(p_ready, 1)

                def p_turn(b, m):
                    p_rows(b, m)
                    p_keep(b, m)

                turns_of_two(act, p_turn)
                act.wait_ge(p_ready, done(NTURNS))
                act.dma_start(p_table.rearrange("(p t) d -> p t d", t=NT), xc[:]).then_inc(ptab_out, 16)
                nc.scalar.activation(wp[0:D, :, :], wts[0:D, C_W1A_BOT:C_W1A_BOT + RING * D].rearrange("p (r d) -> p r d", d=D),
                                     ACT.Copy).then_inc(wc_ready, 1)
                act.wait_ge(wc_raw, 1)
                nc.scalar.activation(wc[:], c_ps[0][0:W, 0:D], ACT.Copy).then_inc(wc_ready, 1)

                def main(summed):
                    def relu(b, g):
                        act.wait_ge(summed, done(g + 1))
                        nc.scalar.activation(rr[:, b, :, 0:D], z_ps[b][:, 0:TPG * D].rearrange("p (t d) -> p t d", d=D),
                                             ACT.Relu).then_inc(relu_ready, 1)

                    relu(0, 0)
                    with act.Fori(0, TURNS) as i:
                        for s in range(RING):
                            g = i * RING + s
                            act.wait_ge(comb_ready, done(g + 1))
                            act.wait_ge(groups_ended, done(g - RING + 1))
                            nc.scalar.activation(vv[:, s, :, :], c_ps[s % 2][:, 0:TPG * W].rearrange("p (t w) -> p t w", w=W),
                                                 ACT.Copy).then_inc(rows_ready, 1)
                            relu((s + 1) % 2, g + 1)

                act.wait_ge(flag_ready, 1)
                fit = act.value_load(fits_i[0:1, 0:1], min_val=0, max_val=1)
                with act.If(fit == 1):
                    main(z_ready)
                with act.Else():
                    main(zsum_ready)

                def mlp(b, m):
                    act.wait_ge(at_raw, done(m + 1))
                    act.wait_ge(hid_raw, done(m - 1))
                    nc.scalar.activation(at_st[:, b, :], srcs_ps[b][0:W, :], ACT.Copy).then_inc(at_ready, 1)
                    act.wait_ge(hid_raw, done(m + 1))
                    act.wait_ge(res_raw, done(m - 1))
                    nc.scalar.activation(hid_st[0:D, b, :], z_ps[b][0:D, :], ACT.Relu).then_inc(hid_ready, 1)

                turns_of_two(act, mlp)

            @block.vector
            def _(dve):
                steps = [0]

                def step(ins):
                    steps[0] += 1
                    ins.then_inc(dve_step, 1)
                    dve.wait_ge(dve_step, steps[0])

                for s in (h_ready, onehot_ready, same_ready, zsum_ready, gidx_ready, rank_ready, a_ready, res_ready):
                    dve.sem_inc(s, START)
                nc.vector.memset(epsb[:], EPS).then_inc(ones_ready, 1)
                nc.vector.memset(ones[:], 1.0).then_inc(ones_ready, 1)
                for st in (ht_st, hid_st):
                    nc.vector.memset(st[D:W, :, :], 1.0).then_inc(ones_ready, 1)
                nc.vector.memset(rr[:, :, :, D:W], 1.0).then_inc(ones_ready, 1)
                dve.wait_ge(x_in, 16)
                step(nc.vector.tensor_reduce(stat[:, 0, :], xs[:], AX.X, ALU.add))
                step(nc.vector.tensor_scalar(stat[:, 0, :], stat[:, 0, :], 1.0 / D, None, ALU.mult))
                mean = stat[:, 0, :].rearrange("p (t a) -> p t a", a=1).to_broadcast([P, NT, D])
                step(nc.vector.tensor_tensor(xc[:], xs[:], mean, ALU.subtract))
                step(nc.vector.tensor_tensor(sq, xc[:], xc[:], ALU.mult))
                nc.vector.tensor_reduce(stat[:, 1, :], sq, AX.X, ALU.add).then_inc(var_ready, 1)
                dve.wait_ge(std_ready, 1)
                step(nc.vector.reciprocal(stat[:, 0, :], stat[:, 2, :]))

                def norm(b, m):
                    dve.wait_ge(ht_raw, done(m - 1))
                    rstd = stat[:, 0, bass.ds(m * TPG, TPG)].rearrange("p (t a) -> p t a", a=1).to_broadcast([P, TPG, D])
                    nc.vector.tensor_tensor(h_st[:, b, :, :], xc[:, bass.ds(m * TPG, TPG), :], rstd, ALU.mult).then_inc(h_ready, 1)

                turns_of_two(dve, norm)
                dve.wait_ge(rows_in[0], 16)
                step(nc.vector.tensor_copy(dstf, row_i[0][:]))
                by_group = dstf.rearrange("p (r c) -> p r c", r=RING)
                step(nc.vector.tensor_reduce(glow[:, 0, :], by_group, AX.X, ALU.min))
                nc.vector.tensor_copy(glow_i[:], glow[:, 0, :]).then_inc(bases_ready, 1)
                step(nc.vector.tensor_reduce(glow[:, 1, :], by_group, AX.X, ALU.max))
                for r, at in enumerate((2, 0)):
                    dve.wait_ge(rows_in[r], 16)
                    nc.vector.tensor_scalar(dig_i, row_i[r][:], 7, None, ALU.arith_shift_right)
                    step(nc.vector.tensor_scalar(dig_j, row_i[r][:], P - 1, None, ALU.bitwise_and))
                    nc.vector.tensor_copy(dig_b[:, at, :], dig_i).then_inc(digits_ready, 1)
                    nc.vector.tensor_copy(dig_b[:, at + 1, :], dig_j).then_inc(digits_ready, 1)
                    dve.wait_ge(digits_ready, 2 * r + 2)
                step(nc.vector.tensor_tensor(wide[:], glow[:, 1, :], glow[:, 0, :], ALU.subtract))
                step(nc.vector.tensor_scalar(wide[:], wide[:], float(WIN - 1), None, ALU.is_gt))
                nc.vector.tensor_reduce(wides[:], wide[:], AX.X, ALU.add).then_inc(wides_ready, 1)
                dve.wait_ge(fits_raw, 1)
                step(nc.vector.tensor_scalar(fits[:], c_ps[1][:, 0:1], 0.0, None, ALU.is_equal))
                nc.vector.tensor_copy(fits_i[:], fits[:]).then_inc(flag_ready, 1)
                dve.wait_ge(consts_ready, 9)
                dve.wait_ge(src_in, 16)
                nc.vector.tensor_copy(wlane[:], wlane_i[:])
                nc.vector.tensor_copy(trash[:], trash_i[:])
                step(nc.vector.tensor_copy(srcf[:], ids_i))
                step(nc.vector.tensor_scalar(src_t[:], srcf[:], trash[:, 0:1], None, ALU.subtract))
                dve.wait_ge(base_in, 16)
                step(nc.vector.tensor_copy(basew[:], base_i[:]))
                step(nc.vector.tensor_scalar(basew[:], basew[:], wlane[:, 0:1], fits[:, 0:1], ALU.add, ALU.mult))
                step(nc.vector.tensor_scalar(basew[:], basew[:], 1.0, None, ALU.subtract))

                def compare(slot, g):
                    b = slot % 2
                    dve.wait_ge(ids_ready, done(g + 1))
                    dve.wait_ge(z_ready, done(g - RING + 1))
                    nc.vector.tensor_scalar(et[D:P, slot, :], dsts_ps[b][D:P, :], basew[D:P, bass.ds(g, 1)], None,
                                            ALU.is_equal).then_inc(onehot_ready, 1)
                    dve.wait_ge(comb_ready, done(g - 1))
                    for k in range(TPG):
                        ins = nc.vector.scalar_tensor_tensor(
                            out=same[:, b, k, :], in0=srcs_ps[b][:, k * P:(k + 1) * P],
                            scalar=srcf[:, bass.ds(g * TPG + k, 1)], in1=upto[:], op0=ALU.is_equal, op1=ALU.mult,
                            accum_out=rank[:, b, k:k + 1])
                    ins.then_inc(rank_ready, 1)
                    dve.wait_ge(rank_ready, (g * 2 + 1) + START)
                    nc.vector.scalar_tensor_tensor(out=pick[:, b, :], in0=rank[:, b, :], scalar=1.0,
                                                   in1=src_t[:, bass.ds(g * TPG, TPG)], op0=ALU.is_equal,
                                                   op1=ALU.mult).then_inc(rank_ready, 1)
                    dve.wait_ge(rank_ready, (g * 2 + 2) + START)
                    dve.wait_ge(groups_ended, done(g - RING + 1))
                    nc.vector.tensor_scalar(sidx[:, slot, :], pick[:, b, :], trash[:, 0:1], None, ALU.add).then_inc(same_ready, 1)

                def add(slot, turn, g):
                    b = slot % 2
                    dve.wait_ge(z_ready, done(g + 1))
                    dve.wait_ge(gathered[slot], (turn + 1) * (16 * TPG))
                    z = z_ps[b][:, 0:TPG * D].rearrange("p (t d) -> p t d", d=D)
                    nc.vector.tensor_tensor(z, z, grow[:, slot, :, :], ALU.add).then_inc(zsum_ready, 1)
                    nc.vector.tensor_copy(gidx[:, slot, :], dsti[:, bass.ds((g + RING) * TPG, TPG)]).then_inc(gidx_ready, 1)

                fit = dve.value_load(fits_i[0:1, 0:1], min_val=0, max_val=1)
                with dve.If(fit == 1):
                    compare(0, 0)
                    with dve.Fori(0, TURNS) as i:
                        for s in range(RING):
                            compare((s + 1) % RING, i * RING + s + 1)
                with dve.Else():
                    dve.wait_ge(dst_in, 16)
                    nc.vector.tensor_copy(gidx[:].rearrange("p r t -> p (r t)"), dsti[:, 0:RING * TPG]).then_inc(gidx_ready, 1)
                    compare(0, 0)
                    add(0, 0, 0)
                    with dve.Fori(0, TURNS) as i:
                        for s in range(RING):
                            g = i * RING + s
                            compare((s + 1) % RING, g + 1)
                            add((s + 1) % RING, i + (s + 1) // RING, g + 1)
                dve.wait_ge(sums_in[0], 16)
                for k in range(1, TABLES):
                    dve.wait_ge(sums_in[k], 16)
                    step(nc.vector.tensor_tensor(tab[0][:], tab[0][:], tab[k][:], ALU.add))
                total = tab[0][:].rearrange("p (t w) -> p t w", w=W)
                step(nc.vector.tensor_scalar(stat[:, 1, :], total[:, :, D], 1.0, None, ALU.max))
                step(nc.vector.reciprocal(stat[:, 2, :], stat[:, 1, :]))

                def mean_of(b, m):
                    dve.wait_ge(at_raw, done(m - 1))
                    rcount = stat[:, 2, bass.ds(m * TPG, TPG)].rearrange("p (t a) -> p t a", a=1).to_broadcast([P, TPG, W])
                    nc.vector.tensor_tensor(a_st[:, b, :, :], total[:, bass.ds(m * TPG, TPG), :], rcount, ALU.mult).then_inc(a_ready, 1)

                def result(b, m):
                    dve.wait_ge(res_raw, done(m + 1))
                    nc.vector.tensor_tensor(xc[:, bass.ds(m * TPG, TPG), :],
                                            c_ps[b][:, 0:TPG * D].rearrange("p (t d) -> p t d", d=D),
                                            xs[:, bass.ds(m * TPG, TPG), :], ALU.add).then_inc(res_ready, 1)

                mean_of(0, 0)

                def res_turn(b, m):
                    mean_of(1 - b, m + 1)
                    result(b, m)

                with dve.Fori(0, (NTURNS - 1) // 2) as i:
                    for b in range(2):
                        res_turn(b, i * 2 + b)
                if NTURNS % 2 == 0:
                    res_turn(0, NTURNS - 2)
                result((NTURNS - 1) % 2, NTURNS - 1)

            @block.tensor
            def _(pe):
                for s in (ht_raw, p_raw, ids_ready, z_ready, comb_ready, at_raw, hid_raw, res_raw):
                    pe.sem_inc(s, START)
                pe.wait_ge(consts_ready, 9)
                pe.wait_ge(ones_ready, 5)
                pe.wait_ge(w_in, 16)
                nc.tensor.matmul(c_ps[0][0:W, 0:D], wts[0:D, C_W1B_T:C_W1B_T + W], wts[0:D, C_W2A_BOT:C_W2A_BOT + D],
                                 start=True, stop=True).then_inc(wc_raw, 1)

                def transposes(b, m):
                    pe.wait_ge(h_ready, done(m + 1))
                    pe.wait_ge(ht_ready, done(m - 1))
                    pe.sem_inc(pe_past, 1)
                    for k in range(TPG):
                        t = nc.tensor.transpose(srcs_ps[b][0:D, k * P:(k + 1) * P], h_st[:, b, k, :], ident[:])
                    t.then_inc(ht_raw, 1)

                def p_rows(b, m):
                    pe.wait_ge(ht_ready, done(m + 1))
                    pe.wait_ge(p_ready, done(m - 1))
                    for k in range(TPG):
                        t = nc.tensor.matmul(z_ps[b][:, k * D:(k + 1) * D], ht_st[:, b, k * P:(k + 1) * P],
                                             wts[0:W, C_W1A_TOP:C_W1A_TOP + D], start=True, stop=True)
                    t.then_inc(p_raw, 1)

                def one_ahead(first, second):
                    first(0, 0)
                    with pe.Fori(0, (NTURNS - 1) // 2) as i:
                        for b in range(2):
                            first(1 - b, i * 2 + b + 1)
                            second(b, i * 2 + b)
                    if NTURNS % 2 == 0:
                        first(1, NTURNS - 1)
                        second(0, NTURNS - 2)
                    second((NTURNS - 1) % 2, NTURNS - 1)

                one_ahead(transposes, p_rows)
                pe.wait_ge(wides_ready, 1)
                nc.tensor.matmul(c_ps[1][:, 0:1], ones[:], wides[:], start=True, stop=True).then_inc(fits_raw, 1)
                pe.wait_ge(wc_ready, 2)
                pe.wait_ge(flag_ready, 1)
                pe.wait_ge(p_ready, done(NTURNS))

                def ids(slot, turn, g):
                    b = slot % 2
                    pe.wait_ge(dig_in[slot], (turn + 1) * 16)
                    pe.wait_ge(same_ready, done(g - 1))
                    nc.tensor.matmul(dsts_ps[b][:], spread[:, 1, :], dig[:, slot, :], start=True, stop=True)
                    nc.tensor.matmul(srcs_ps[b][:], spread[:, 0, :], dig[:, slot, :], start=True, stop=True).then_inc(ids_ready, 1)

                def z(slot, turn, g):
                    b = slot % 2
                    pe.wait_ge(et_in[slot], (turn + 1) * 16)
                    pe.wait_ge(wp_in[slot], (turn + 1) * 16)
                    pe.wait_ge(relu_ready, done(g - 1))
                    pe.wait_ge(onehot_ready, done(g + 1))
                    for k in range(TPG):
                        t = nc.tensor.matmul(z_ps[b][:, k * D:(k + 1) * D], et[:, slot, k * P:(k + 1) * P], wp[:, slot, :],
                                             start=True, stop=True)
                    t.then_inc(z_ready, 1)

                def combine(slot, g):
                    b = slot % 2
                    pe.wait_ge(same_ready, done(g + 1))
                    pe.wait_ge(relu_ready, done(g + 1))
                    pe.wait_ge(rows_ready, done(g - 1))
                    for k in range(TPG):
                        t = nc.tensor.matmul(c_ps[b][:, k * W:(k + 1) * W], same[:, b, k, :], rr[:, b, k, :],
                                             start=True, stop=True)
                    t.then_inc(comb_ready, 1)

                ids(0, 0, 0)
                z(0, 0, 0)
                with pe.Fori(0, TURNS) as i:
                    for s in range(RING):
                        g = i * RING + s
                        nxt, turn = (s + 1) % RING, i + (s + 1) // RING
                        ids(nxt, turn, g + 1)
                        combine(s, g)
                        z(nxt, turn, g + 1)
                pe.wait_ge(relu_ready, done(GROUPS + 1))
                pe.wait_ge(same_ready, done(GROUPS + 1))
                pe.wait_ge(ht_kept, done(NTURNS))

                def mean_t(b, m):
                    pe.wait_ge(a_ready, done(m + 1))
                    pe.wait_ge(at_ready, done(m - 1))
                    pe.sem_inc(pe_past, 1)
                    for k in range(TPG):
                        t = nc.tensor.transpose(srcs_ps[b][0:W, k * P:(k + 1) * P], a_st[:, b, k, :], ident[:])
                    t.then_inc(at_raw, 1)

                def mlp(b, m):
                    pe.wait_ge(at_ready, done(m + 1))
                    pe.wait_ge(hid_ready, done(m - 1))
                    nc.tensor.matmul(z_ps[b][0:D, :], wts[0:W, C_W2A_TOP:C_W2A_TOP + D], ht[:, bass.ds(m * GE, GE)],
                                     start=True, stop=False)
                    nc.tensor.matmul(z_ps[b][0:D, :], wc[:], at_st[:, b, :], start=False, stop=True).then_inc(hid_raw, 1)
                    pe.wait_ge(hid_ready, done(m + 1))
                    pe.wait_ge(res_ready, done(m - 1))
                    for k in range(TPG):
                        t = nc.tensor.matmul(c_ps[b][:, k * D:(k + 1) * D], hid_st[:, b, k * P:(k + 1) * P],
                                             wts[0:W, C_W2B:C_W2B + D], start=True, stop=True)
                    t.then_inc(res_raw, 1)

                one_ahead(mean_t, mlp)


def kernel(x, src, dst, edge_attr_64, L0_gnn_u, L0_gnn_W1a, L0_gnn_b1a, L0_gnn_W1b, L0_gnn_b1b, L0_gnn_W2a, L0_gnn_b2a,
           L0_gnn_W2b, L0_gnn_b2b):
    import numpy as np
    import concourse.bacc as bacc
    from concourse.bass_utils import run_bass_kernel_spmd

    more = EDGES - N_EDGES
    e_t = np.pad(np.asarray(edge_attr_64), ((0, more), (0, 0))).T
    src_p = np.pad(np.asarray(src), (0, more), constant_values=PAD_NODE)
    dst_p = np.pad(np.asarray(dst), (0, more), mode="edge")
    w1a, w1b, w2a, w2b = (np.asarray(w) for w in (L0_gnn_W1a, L0_gnn_W1b, L0_gnn_W2a, L0_gnn_W2b))
    b1a, b1b, b2a, b2b = (np.asarray(b)[None] for b in (L0_gnn_b1a, L0_gnn_b1b, L0_gnn_b2a, L0_gnn_b2b))
    parts = [np.concatenate([w1a[:D], b1a])] + [w1a[D:]] * RING + [np.concatenate([w1b, b1b]).T, np.concatenate([w2a[:D], b2a]), w2a[D:],
                                                                  np.concatenate([w2b, b2b])]
    arrays = {
        "x": np.pad(np.asarray(x), ((0, NODES - N_NODES), (0, 0))),
        "e_t": e_t,
        "src_col": src_p.reshape(COLS, P).T, "dst_col": dst_p.reshape(COLS, P).T,
        "src_row": src_p.reshape(ROWP, RING * GE), "dst_row": dst_p.reshape(ROWP, RING * GE),
        "weights": np.concatenate([np.pad(p, ((0, P - len(p)), (0, 0))) for p in parts], axis=1),
    }
    arrays = {"in_" + n: np.ascontiguousarray(a) for n, a in arrays.items()}
    nc = bacc.Bacc("TRN2", target_bir_lowering=False, num_devices=1)
    args = [nc.dram_tensor(n, a.shape, mybir.dt.from_np(a.dtype), kind="ExternalInput").ap() for n, a in arrays.items()]
    out = nc.dram_tensor("out_0", (N_NODES, D), mybir.dt.float32, kind="ExternalOutput").ap()
    gnn_kernel(nc, *args, out)
    r = run_bass_kernel_spmd(nc, [arrays], core_ids=[0])
    return r.results[0]["out_0"]
```

```python
import concourse.bass as bass
from concourse import mybir
from contextlib import ExitStack
from functools import partial

N_NODES, D, N_EDGES = 6250, 64, 200000
P = 128
TPG = 4
GE = P * TPG
RING = 6
GROUPS = -(-N_EDGES // GE)
TURNS = GROUPS // RING
LEFT = GROUPS % RING
ROWG = 4
ROWP = -(-(GROUPS + RING) // ROWG)
ALL = ROWP * ROWG
EDGES = ALL * GE
COLS = EDGES // P
NT = -(-N_NODES // P)
NT += -NT % TPG
NTURNS = NT // TPG
NODES = NT * P
W = D + 1
PAD_NODE = N_NODES
TRASH = N_NODES + 1
TABLES = 6
LAG = -(-TABLES // TPG)
WIN = P - D
START = RING + 1
EPS = 1e-5

C_W1A_TOP = 0
C_W1A_BOT = C_W1A_TOP + D
C_W1B_T = C_W1A_BOT + D
C_W2A_TOP = C_W1B_T + W
C_W2A_BOT = C_W2A_TOP + D
C_W2B = C_W2A_BOT + D
WCOLS = C_W2B + D


CHUNKS = [(0, 2), (2, 5), (5, 9), (9, NTURNS)]


X_PARTS = [(0, 4), (4, NTURNS)]
OUT_PARTS = [(0, 8), (8, NTURNS - 1), (NTURNS - 1, NTURNS)]
P_PARTS = [(0, 6), (6, NTURNS - 2), (NTURNS - 2, NTURNS)]


def done(n):
    return n + START


def gnn_kernel(nc, x, e_t, src_col, dst_col, src_row, dst_row, weights, out):
    f32, i32, u8, bf16 = mybir.dt.float32, mybir.dt.int32, mybir.dt.uint8, mybir.dt.bfloat16
    ALU, ACT, AX = mybir.AluOpType, mybir.ActivationFunctionType, mybir.AxisListType
    assert TRASH + P <= NODES and RING * TPG % TABLES == 0 and RING % 2 == 0 and NTURNS % 4 == 1

    with ExitStack() as ctx:
        def sb(name, shape, dt=f32):
            return ctx.enter_context(nc.sbuf_tensor(name, shape, dt))

        def pb(name, shape, dt=f32):
            return ctx.enter_context(nc.psum_tensor(name, shape, dt))

        def sem(name):
            return ctx.enter_context(nc.semaphore(name))

        p_table = nc.dram_tensor("p_table", [NODES, D], f32).ap()
        digits = nc.dram_tensor("digits", [4, EDGES], bf16).ap()
        bases = nc.dram_tensor("bases", [1, ALL], i32).ap()
        sums = [nc.dram_tensor(f"sums{k}", [NODES, W], f32).ap() for k in range(TABLES)]

        ident = sb("ident", [P, P])
        upto = sb("upto", [P, P])
        spread = sb("spread", [4, 2, P], bf16)
        wts = sb("wts", [P, WCOLS])
        wc = sb("wc", [W, D])
        trash_i = sb("trash_i", [P, 1], i32)
        trash = sb("trash", [P, 1])
        untrash = sb("untrash", [P, 1])
        epsb = sb("epsb", [P, 1])
        first_root = sb("first_root", [P, 1])
        ones = sb("ones", [ROWP, P])

        xs = sb("xs", [P, NT, D])
        xc = sb("xc", [P, NT, D])
        stat = sb("stat", [P, 3, NT])
        h_st = sb("h_st", [P, 2, TPG, D])
        ht_st = sb("ht_st", [W, 2, GE])
        ht = sb("ht", [W, NODES])
        tab = [sb(f"tab{k}", [P, NT * W]) for k in range(TABLES)]
        a_st = sb("a_st", [P, 2, TPG, W])
        at_st = sb("at_st", [W, 2, GE])
        hid_st = ht_st
        sq = tab[5][:, 0:NT * D].rearrange("p (t d) -> p t d", d=D)

        srcf = sb("srcf", [P, COLS])
        src_t = sb("src_t", [P, COLS])
        dsti = tab[5][:, 0:COLS].bitcast(i32)
        basew = sb("basew", [P, ALL])
        base_i = sb("base_i", [P, ALL], i32)
        wlane_i = sb("wlane_i", [P, 1], i32)
        wlane = sb("wlane", [P, 1])
        glow = sb("glow", [ROWP, 2, ROWG])
        glow_i = sb("glow_i", [ROWP, ROWG], i32)
        wide = sb("wide", [ROWP, ROWG])
        wides = sb("wides", [ROWP, 1])
        fits = sb("fits", [P, 1])
        fits_i = sb("fits_i", [P, 1], i32)
        ids_i = src_t[:].bitcast(i32)
        row_i = [tab[1 + r][0:ROWP, 0:ROWG * GE].bitcast(i32) for r in range(2)]
        row_bytes = [tab[1 + r][0:ROWP, 0:ROWG * GE].bitcast(u8).rearrange("p (c b) -> p b c", b=4)[:, 0:2, :] for r in range(2)]
        row_d = [tab[3 + r][0:ROWP, 0:ROWG * GE].bitcast(bf16).rearrange("p (d c) -> p d c", d=2) for r in range(2)]

        et = sb("et", [P, RING, GE])
        wp = sb("wp", [P, RING, D])
        dig = sb("dig", [4, RING, GE], bf16)
        gidx = sb("gidx", [P, RING, TPG], i32)
        grow = sb("grow", [P, RING, TPG, D])
        same = sb("same", [P, 2, TPG, P], bf16)
        rank = sb("rank", [P, 2, TPG])
        pick = sb("pick", [P, 2, TPG])
        sidx = sb("sidx", [P, RING, TPG], i32)
        rr = sb("rr", [P, 2, TPG, D])
        r_hi = sb("r_hi", [P, 2, TPG, W], bf16)
        r_mid = sb("r_mid", [P, 2, TPG, D], bf16)
        r_lo = sb("r_lo", [P, 2, TPG, D], bf16)
        vv = sb("vv", [P, RING, TPG, W])

        srcs_ps = [pb(f"srcs_ps{b}", [P, 512]) for b in range(2)]
        dsts_ps = pb("dsts_ps", [P, 512])
        u_ps = pb("u_ps", [P, 512])
        z_ps = [pb(f"z_ps{b}", [P, 512]) for b in range(2)]
        c_ps = [pb(f"c_ps{b}", [P, 512]) for b in range(2)]

        x_in = [sem(f"x_in{k}") for k in range(len(X_PARTS))]
        sum_ready, xc_ready, sq_ready, rstd_ready = (sem(n) for n in ("sum_ready", "xc_ready", "sq_ready", "rstd_ready"))
        (w_in, src_in, dst_in, rows_in0, rows_in1, digits_out, bases_out, base_in, base_row_in, ptab_out,
         res_out) = (
            sem(n) for n in ("w_in", "src_in", "dst_in", "rows_in0", "rows_in1", "digits_out", "bases_out",
                             "base_in", "base_row_in", "ptab_out", "res_out"))
        sums_in = [sem(f"sums_in{c}") for c in range(len(CHUNKS))]
        rows_in = [rows_in0, rows_in1]
        digits_ready = [sem(f"digits_ready{r}") for r in range(2)]
        zeros_ready, consts_ready, ones_ready, src_ready, bases_ready, wides_ready, fits_raw, flag_ready, wc_raw, wc_ready = (
            sem(n) for n in ("zeros_ready", "consts_ready", "ones_ready", "src_ready", "bases_ready", "wides_ready",
                             "fits_raw", "flag_ready", "wc_raw", "wc_ready"))
        pool_sum, ht_ones = sem("pool_sum"), sem("ht_ones")
        rest_ready, mid_ready, parts_ready, dve_step, var_ready, std_ready, pool_past, pe_past = (
            sem(n) for n in ("rest_ready", "mid_ready", "parts_ready", "dve_step", "var_ready", "std_ready", "pool_past", "pe_past"))
        h_ready, ht_raw, ht_ready, ht_kept, p_raw, p_ready = (
            sem(n) for n in ("h_ready", "ht_raw", "ht_ready", "ht_kept", "p_raw", "p_ready"))
        et_in, wp_in, dig_in, gathered = ([sem(f"{n}{s}") for s in range(RING)] for n in ("et_in", "wp_in", "dig_in", "gathered"))
        scattered = [sem(f"scattered{k}") for k in range(TABLES)]
        ids_ready, onehot_ready, same_ready, z_ready, zsum_ready, gidx_ready, relu_ready, comb_ready, rows_ready, groups_ended, rank_ready = (
            sem(n) for n in ("ids_ready", "onehot_ready", "same_ready", "z_ready", "zsum_ready", "gidx_ready", "relu_ready",
                             "comb_ready", "rows_ready", "groups_ended", "rank_ready"))
        tables_in, added_1, added_2, added_3, counts_ready, inverse_ready, hsum_ready, u_raw, u_ready, a_ready, at_raw, at_ready, hid_raw, hid_ready, res_raw, res_ready = (
            sem(n) for n in ("tables_in", "added_1", "added_2", "added_3", "counts_ready", "inverse_ready", "hsum_ready", "u_raw", "u_ready", "a_ready", "at_raw", "at_ready", "hid_raw", "hid_ready", "res_raw", "res_ready"))

        def ended(t):
            return 16 * (1 + len(range(t, GROUPS * TPG, TABLES)))

        def main_loop(eng, step, beside=None):
            def turns(first, last, beside):
                with eng.Fori(first, last) as i:
                    for s in range(RING):
                        step(s, i, i * RING + s)
                        if beside and s == RING - 1:
                            beside(i)
            if beside:
                turns(0, NTURNS, beside)
            turns(NTURNS if beside else 0, TURNS, None)
            for s in range(LEFT):
                step(s, TURNS, TURNS * RING + s)

        def pipelined(eng, stages):
            far = max(lead for lead, _ in stages)

            def step(b, t, low=0, high=0):
                for lead, stage in stages:
                    if low + lead >= 0 and high + lead < NTURNS:
                        stage((b + lead) % 2, t + lead)

            for t in range(-far, 0):
                step(t % 2, t, t, t)
            pairs = (NTURNS - far) // 2
            with eng.Fori(0, pairs) as i:
                for b in range(2):
                    step(b, i * 2 + b)
            for t in range(2 * pairs, NTURNS):
                step(t % 2, t, t, t)

        with nc.Block() as block:

            @block.sync
            def _(sp):
                x_rows = x.rearrange("(p t) d -> p t d", t=NT)
                sp.dma_start(row_i[0], dst_row).then_inc(rows_in[0], 16)
                for k, (m, n) in enumerate(X_PARTS):
                    sp.dma_start(xs[:, m * TPG:n * TPG, :], x_rows[:, m * TPG:n * TPG, :]).then_inc(x_in[k], 16)
                    if k == 0:
                        sp.dma_start(wts[:], weights).then_inc(w_in, 16)
                        sp.dma_start(row_i[1], src_row).then_inc(rows_in[1], 16)
                sp.dma_start(ids_i, src_col).then_inc(src_in, 16)
                for s in range(RING):
                    sp.dma_start(et[0:D, s, :], e_t[:, s * GE:(s + 1) * GE]).then_inc(et_in[s], 16)
                sp.wait_ge(bases_ready, 1)
                sp.dma_start(bases.rearrange("a (p r) -> (a p) r", r=ROWG), glow_i[:]).then_inc(bases_out, 16)
                sp.wait_ge(bases_out, 16)
                sp.dma_start(base_i[:], bases.to_broadcast([P, ALL])).then_inc(base_in, 16)
                table = p_table.rearrange("(p t) d -> p t d", t=NT)

                def store_p(m, n):
                    sp.wait_ge(p_ready, done(n))
                    sp.dma_start(table[:, m * TPG:n * TPG, :], xc[:, m * TPG:n * TPG, :]).then_inc(ptab_out, 16)

                store_p(*P_PARTS[0])
                for r, at in enumerate((2, 0)):
                    sp.wait_ge(digits_ready[r], 1)
                    sp.dma_start(digits[at:at + 2].rearrange("d (p c) -> p d c", p=ROWP), row_d[r]).then_inc(digits_out, 16)
                def load_digits(slot, g):
                    sp.dma_start(dig[:, slot, :], digits[:, bass.ds(g * GE, GE)]).then_inc(dig_in[slot], 16)

                def window(g):
                    return sp.value_load(base_i[0:1, bass.ds(g, 1)], min_val=0, max_val=N_NODES - 1)

                def load_window(slot, base):
                    sp.dma_start(wp[D:P, slot, :], p_table[bass.ds(base, WIN), :]).then_inc(wp_in[slot], 16)

                sp.wait_ge(base_in, 16)
                first = [window(s) for s in range(RING)]
                store_p(*P_PARTS[1])
                sp.wait_ge(digits_out, 32)
                for s in range(RING):
                    load_digits(s, s)
                store_p(*P_PARTS[2])
                sp.wait_ge(ptab_out, 16 * len(P_PARTS))
                for s in range(RING):
                    load_window(s, first[s])
                with sp.Fori(0, TURNS) as i:
                    for s in range(RING):
                        g = i * RING + s
                        sp.wait_ge(z_ready, done(g + 1))
                        load_digits(s, g + RING)
                        load_window(s, window(g + RING))
                        sp.dma_start(et[0:D, s, :], e_t[:, bass.ds((g + RING) * GE, GE)]).then_inc(et_in[s], 16)
                for s in range(RING):
                    for ring in (et_in, wp_in, dig_in):
                        sp.wait_ge(ring[s], 16 * (TURNS + 1))
                sp.wait_ge(relu_ready, done(GROUPS + 1))
                for t in range(TABLES):
                    sp.wait_ge(scattered[t], ended(t))
                sp.sem_inc(tables_in, START)
                for c, (m, n) in enumerate(CHUNKS + [(NTURNS, NTURNS)]):
                    for t in range(TABLES):
                        if m < n:
                            sp.dma_start(tab[t][:, m * TPG * W:n * TPG * W],
                                         sums[t].rearrange("(p t) w -> p (t w)", t=NT)[:, m * TPG * W:n * TPG * W]
                                         ).then_inc(sums_in[c], 16)
                    if c > 0:
                        sp.wait_ge(sums_in[c - 1], 16 * TABLES)
                        sp.sem_inc(tables_in, CHUNKS[c - 1][1] - CHUNKS[c - 1][0])
                full = N_NODES // NT
                rest = N_NODES - full * NT
                rows = out[0:full * NT, :].rearrange("(p t) d -> p t d", t=NT)
                for m, n in OUT_PARTS:
                    sp.wait_ge(res_ready, done(n))
                    sp.dma_start(rows[:, m * TPG:n * TPG, :], xc[0:full, m * TPG:n * TPG, :]).then_inc(res_out, 16)
                    if m == 0:
                        sp.dma_start(out[full * NT:, :].rearrange("(p t) d -> p t d", t=rest),
                                     xc[full:full + 1, 0:rest, :]).then_inc(res_out, 16)
                sp.wait_ge(res_out, 16 * (len(OUT_PARTS) + 1))

            @block.gpsimd
            def _(pool):
                nc.gpsimd.memset(ident[:], 0.0).then_inc(consts_ready, 1)
                nc.gpsimd.memset(upto[:], 1.0).then_inc(consts_ready, 1)
                nc.gpsimd.iota(trash_i[:], pattern=[[0, 1]], base=TRASH, channel_multiplier=1).then_inc(consts_ready, 1)
                nc.gpsimd.iota(wlane_i[:], pattern=[[0, 1]], base=1 - D, channel_multiplier=1).then_inc(consts_ready, 1)
                nc.gpsimd.memset(spread[:], 0.0).then_inc(consts_ready, 1)
                pool.wait_ge(consts_ready, 5)
                nc.gpsimd.affine_select(out=ident[:], in_=ident[:], compare_op=ALU.not_equal, fill=1.0, base=0,
                                        pattern=[[-1, P]], channel_multiplier=1).then_inc(consts_ready, 1)
                nc.gpsimd.affine_select(out=upto[:], in_=upto[:], compare_op=ALU.is_ge, fill=0.0, base=0,
                                        pattern=[[-1, P]], channel_multiplier=1).then_inc(consts_ready, 1)
                nc.gpsimd.affine_select(out=spread[:], in_=spread[:], compare_op=ALU.not_equal, fill=1.0, base=0,
                                        pattern=[[-2, 2], [0, P]], channel_multiplier=1).then_inc(consts_ready, 1)
                pool.wait_ge(consts_ready, 8)
                nc.gpsimd.affine_select(out=spread[:], in_=spread[:], compare_op=ALU.not_equal, fill=256.0, base=-1,
                                        pattern=[[-2, 2], [0, P]], channel_multiplier=1).then_inc(consts_ready, 1)
                nc.gpsimd.tensor_copy(trash[:], trash_i[:]).then_inc(consts_ready, 1)
                nc.gpsimd.tensor_copy(wlane[:], wlane_i[:]).then_inc(consts_ready, 1)
                pool.wait_ge(consts_ready, 11)
                nc.gpsimd.tensor_scalar(untrash[:], trash[:], -1.0, None, ALU.mult).then_inc(consts_ready, 1)
                nc.gpsimd.memset(tab[0][:], 0.0).then_inc(zeros_ready, 1)
                pool.wait_ge(zeros_ready, 1)
                for part in x_in:
                    pool.wait_ge(part, 16)
                def zero(k):
                    pool.dma_start(sums[k].rearrange("(p t) w -> p (t w)", t=NT), tab[0][:]).then_inc(scattered[k], 16)

                for k in range(TABLES - 2):
                    zero(k)
                pool.wait_ge(consts_ready, 12)
                pool.wait_ge(rows_in[1], 16)
                nc.gpsimd.tensor_copy(row_d[1], row_bytes[1]).then_inc(digits_ready[1], 1)
                pool.wait_ge(digits_ready[1], 1)
                nc.gpsimd.memset(ht[D:W, :], 1.0).then_inc(ht_ones, 1)

                def gather(slot):
                    for k in range(TPG):
                        nc.gpsimd.indirect_dma_start(
                            out=grow[:, slot, k, :], out_offset=None, in_=p_table[:, :],
                            in_offset=bass.IndirectOffsetOnAxis(ap=gidx[:, slot, k:k + 1], axis=0),
                        ).then_inc(gathered[slot], 16)

                def scatter(slot, turn, g):
                    for k in range(TPG):
                        before, t = divmod(slot * TPG + k, TABLES)
                        if k == 0:
                            pool.wait_ge(same_ready, done(g + 1))
                            pool.wait_ge(rows_ready, done(g + 1))
                        pool.wait_ge(scattered[t], (turn * (RING * TPG // TABLES) + before + 1) * 16)
                        pool.sem_inc(pool_past, 1)
                        nc.gpsimd.indirect_dma_start(
                            out=sums[t][:, :],
                            out_offset=bass.IndirectOffsetOnAxis(ap=sidx[:, slot, k:k + 1], axis=0),
                            in_=vv[:, slot, k, :], in_offset=None, compute_op=ALU.add,
                        ).then_inc(scattered[t], 16)
                    pool.sem_inc(groups_ended, 1)

                pool.sem_inc(groups_ended, START - LAG)
                pool.wait_ge(ht_ones, 1)
                pool.wait_ge(wp_in[RING - 1], 16)
                for k in range(TABLES - 2, TABLES):
                    zero(k)
                pool.wait_ge(flag_ready, 1)
                fit = pool.value_load(fits_i[0:1, 0:1], min_val=0, max_val=1)
                with pool.If(fit == 1):
                    main_loop(pool, scatter)
                with pool.Else():
                    pool.dma_start(dsti, dst_col).then_inc(dst_in, 16)
                    pool.wait_ge(ptab_out, 16 * len(P_PARTS))
                    pool.wait_ge(gidx_ready, done(1))
                    for s in range(RING - 1):
                        gather(s)

                    def both(slot, turn, g):
                        pool.wait_ge(gidx_ready, done(g + 1))
                        pool.wait_ge(zsum_ready, done(g))
                        pool.sem_inc(pool_past, 1)
                        gather((slot + RING - 1) % RING)
                        scatter(slot, turn, g)

                    main_loop(pool, both)
                    for s in range(RING):
                        pool.wait_ge(gathered[s], 16 * TPG * len(range(s, GROUPS + RING - 1, RING)))
                pool.sem_inc(pool_sum, START)
                with pool.Fori(0, NTURNS) as m:
                    part = bass.ds(m * (TPG * W), TPG * W)
                    pool.wait_ge(tables_in, done(m + 1))
                    nc.gpsimd.tensor_tensor(tab[3][:, part], tab[3][:, part], tab[4][:, part], ALU.add).then_inc(pool_sum, 1)
                    pool.wait_ge(pool_sum, done(m * 2 + 1))
                    nc.gpsimd.tensor_tensor(tab[3][:, part], tab[3][:, part], tab[5][:, part], ALU.add).then_inc(pool_sum, 1)

            @block.scalar
            def _(act):
                act.sem_inc(ht_ready, START)
                act.sem_inc(ht_kept, START)
                act.sem_inc(relu_ready, START)
                act.sem_inc(mid_ready, START)
                act.sem_inc(rows_ready, START)
                act.sem_inc(at_ready, START)
                act.sem_inc(hid_ready, START)
                act.sem_inc(u_ready, START)
                act.sem_inc(sq_ready, START)
                act.sem_inc(std_ready, START)
                act.wait_ge(rows_in[0], 16)
                nc.scalar.activation(row_d[0], row_bytes[0], ACT.Copy).then_inc(digits_ready[0], 1)
                act.wait_ge(ones_ready, 4)
                nc.scalar.activation(first_root[:], epsb[:], ACT.Sqrt)

                def square(b, m):
                    act.wait_ge(xc_ready, done(m + 1))
                    nc.scalar.activation(sq[:, bass.ds(m * TPG, TPG), :], xc[:, bass.ds(m * TPG, TPG), :],
                                         ACT.Square).then_inc(sq_ready, 1)

                def root(b, m):
                    act.wait_ge(var_ready, done(m + 1))
                    nc.scalar.activation(stat[:, 2, bass.ds(m * TPG, TPG)], stat[:, 1, bass.ds(m * TPG, TPG)], ACT.Sqrt,
                                         bias=epsb[:], scale=1.0 / D).then_inc(std_ready, 1)

                def h_keep(b, m):
                    act.wait_ge(ht_raw, done(m + 1))
                    act.wait_ge(p_raw, done(m - 1))
                    nc.scalar.activation(ht_st[0:D, b, :], srcs_ps[b][0:D, :], ACT.Relu).then_inc(ht_ready, 1)
                    nc.scalar.activation(ht[0:D, bass.ds(m * GE, GE)], srcs_ps[b][0:D, :], ACT.Relu).then_inc(ht_kept, 1)

                pipelined(act, [(1, h_keep), (5, square), (4, root)])
                act.wait_ge(src_in, 16)
                nc.scalar.activation(srcf[:], ids_i, ACT.Copy).then_inc(src_ready, 1)
                act.wait_ge(src_ready, 1)
                act.wait_ge(consts_ready, 12)
                nc.scalar.activation(src_t[:], srcf[:], ACT.Identity, bias=untrash[:]).then_inc(src_ready, 1)
                act.wait_ge(w_in, 16)
                bottom = wts[0:D, C_W1A_BOT:C_W1A_BOT + D].rearrange("p (r d) -> p r d", r=1).to_broadcast([D, RING, D])
                nc.scalar.activation(wp[0:D, :, :], bottom, ACT.Copy).then_inc(wc_ready, 1)
                act.wait_ge(wc_raw, 1)
                nc.scalar.activation(wc[:], c_ps[0][0:W, 0:D], ACT.Copy).then_inc(wc_ready, 1)

                def main(summed):
                    def relu(b, g):
                        z = z_ps[b][:, 0:TPG * D].rearrange("p (t d) -> p t d", d=D)
                        act.wait_ge(summed, done(g + 1))
                        act.wait_ge(parts_ready, done(g - 1))
                        nc.scalar.activation(rr[:, b, :, :], z, ACT.Relu)
                        act.wait_ge(comb_ready, done(g - 1))
                        nc.scalar.activation(r_hi[:, b, :, 0:D], z, ACT.Relu).then_inc(relu_ready, 1)

                    def mid(b, g):
                        act.wait_ge(rest_ready, done(g + 1))
                        nc.scalar.activation(r_mid[:, b, :, :], rr[:, b, :, :], ACT.Copy).then_inc(mid_ready, 1)

                    def step(slot, turn, g):
                        relu((slot + 1) % 2, g + 1)
                        act.wait_ge(comb_ready, done(g + 1))
                        act.wait_ge(groups_ended, done(g - RING + 1))
                        nc.scalar.activation(vv[:, slot, :, :], c_ps[slot % 2][:, 0:TPG * W].rearrange("p (t w) -> p t w", w=W),
                                             ACT.Copy).then_inc(rows_ready, 1)
                        mid((slot + 1) % 2, g + 1)

                    def u_keep(i):
                        act.wait_ge(u_raw, done(i + 1))
                        nc.scalar.activation(ht[0:D, bass.ds(i * GE, GE)], u_ps[0:D, :], ACT.Copy).then_inc(u_ready, 1)

                    relu(0, 0)
                    mid(0, 0)
                    main_loop(act, step, u_keep)

                act.wait_ge(flag_ready, 1)
                fit = act.value_load(fits_i[0:1, 0:1], min_val=0, max_val=1)
                with act.If(fit == 1):
                    main(z_ready)
                with act.Else():
                    main(zsum_ready)

                def mean_t_keep(b, m):
                    act.wait_ge(at_raw, done(m + 1))
                    act.wait_ge(hid_raw, done(m - 1))
                    nc.scalar.activation(at_st[:, b, :], srcs_ps[b][0:W, :], ACT.Copy).then_inc(at_ready, 1)

                def hidden(b, m):
                    act.wait_ge(hsum_ready, done(m + 1))
                    nc.scalar.activation(hid_st[0:D, b, :], hid_st[0:D, b, :], ACT.Relu).then_inc(hid_ready, 1)

                pipelined(act, [(1, hidden), (2, mean_t_keep)])

            @block.vector
            def _(dve):
                steps = [0]

                def step(ins):
                    steps[0] += 1
                    ins.then_inc(dve_step, 1)
                    dve.wait_ge(dve_step, steps[0])

                for s in (sum_ready, xc_ready, var_ready, rstd_ready, h_ready, p_ready, onehot_ready, same_ready, zsum_ready, gidx_ready, rank_ready, rest_ready, parts_ready, a_ready, hsum_ready, res_ready,
                          added_1, added_2, added_3, counts_ready, inverse_ready):
                    dve.sem_inc(s, START)
                nc.vector.memset(epsb[:], EPS).then_inc(ones_ready, 1)
                nc.vector.memset(ones[:], 1.0).then_inc(ones_ready, 1)
                nc.vector.memset(ht_st[D:W, :, :], 1.0).then_inc(ones_ready, 1)
                nc.vector.memset(r_hi[:, :, :, D:W], 1.0).then_inc(ones_ready, 1)
                dve.wait_ge(rows_in[0], 16)
                by_group = row_i[0].rearrange("p (r c) -> p r c", r=ROWG)
                step(nc.vector.tensor_reduce(glow[:, 0, :], by_group, AX.X, ALU.min))
                nc.vector.tensor_copy(glow_i[:], glow[:, 0, :]).then_inc(bases_ready, 1)
                step(nc.vector.tensor_reduce(glow[:, 1, :], by_group, AX.X, ALU.max))
                step(nc.vector.tensor_tensor(wide[:], glow[:, 1, :], glow[:, 0, :], ALU.subtract))
                step(nc.vector.tensor_scalar(wide[:], wide[:], float(WIN - 1), None, ALU.is_gt))
                nc.vector.tensor_reduce(wides[:], wide[:], AX.X, ALU.add).then_inc(wides_ready, 1)

                def of(m, k):
                    return stat[:, k, bass.ds(m * TPG, TPG)]

                def on_rows(m, k):
                    return of(m, k).rearrange("p (t a) -> p t a", a=1).to_broadcast([P, TPG, D])

                def row_sum(b, m):
                    for part, (first, _) in zip(x_in, X_PARTS):
                        if isinstance(m, int) and m == first:
                            dve.wait_ge(part, 16)
                    nc.vector.tensor_reduce(of(m, 0), xs[:, bass.ds(m * TPG, TPG), :], AX.X, ALU.add).then_inc(sum_ready, 1)

                def centre(b, m):
                    dve.wait_ge(sum_ready, done(m + 1))
                    nc.vector.scalar_tensor_tensor(out=xc[:, bass.ds(m * TPG, TPG), :], in0=on_rows(m, 0), scalar=-1.0 / D,
                                                   in1=xs[:, bass.ds(m * TPG, TPG), :], op0=ALU.mult,
                                                   op1=ALU.add).then_inc(xc_ready, 1)

                def square_sum(b, m):
                    dve.wait_ge(sq_ready, done(m + 1))
                    nc.vector.tensor_reduce(of(m, 1), sq[:, bass.ds(m * TPG, TPG), :], AX.X, ALU.add).then_inc(var_ready, 1)

                def rstd(b, m):
                    dve.wait_ge(std_ready, done(m + 1))
                    nc.vector.reciprocal(of(m, 0), of(m, 2)).then_inc(rstd_ready, 1)

                def norm(b, m):
                    dve.wait_ge(rstd_ready, done(m + 1))
                    dve.wait_ge(ht_raw, done(m - 1))
                    nc.vector.tensor_tensor(h_st[:, b, :, :], xc[:, bass.ds(m * TPG, TPG), :], on_rows(m, 0),
                                            ALU.mult).then_inc(h_ready, 1)

                def p_keep(b, m):
                    dve.wait_ge(p_raw, done(m + 1))
                    nc.vector.tensor_scalar(xc[:, bass.ds(m * TPG, TPG), :],
                                            z_ps[b][:, 0:TPG * D].rearrange("p (t d) -> p t d", d=D), 1.0, None,
                                            ALU.mult).then_inc(p_ready, 1)

                pipelined(dve, [(2, norm), (3, rstd), (4, square_sum), (5, centre), (6, row_sum), (0, p_keep)])
                dve.wait_ge(fits_raw, 1)
                step(nc.vector.tensor_scalar(fits[:], c_ps[1][:, 0:1], 0.0, None, ALU.is_equal))
                nc.vector.tensor_copy(fits_i[:], fits[:]).then_inc(flag_ready, 1)
                dve.wait_ge(consts_ready, 12)
                dve.wait_ge(src_ready, 2)
                dve.wait_ge(base_in, 16)
                step(nc.vector.tensor_copy(basew[:], base_i[:]))
                step(nc.vector.tensor_scalar(basew[:], basew[:], wlane[:, 0:1], fits[:, 0:1], ALU.add, ALU.mult))
                step(nc.vector.tensor_scalar(basew[:], basew[:], 1.0, None, ALU.subtract))

                def one_hot(slot, g):
                    dve.wait_ge(ids_ready, done(g + 1))
                    dve.wait_ge(z_ready, done(g - RING + 1))
                    nc.vector.tensor_scalar(et[D:P, slot, :], dsts_ps[D:P, :], basew[D:P, bass.ds(g, 1)], None,
                                            ALU.is_equal).then_inc(onehot_ready, 1)

                def same_src(slot, g):
                    b = slot % 2
                    dve.wait_ge(comb_ready, done(g - 1))
                    for k in range(TPG):
                        ins = nc.vector.scalar_tensor_tensor(
                            out=same[:, b, k, :], in0=srcs_ps[b][:, k * P:(k + 1) * P],
                            scalar=srcf[:, bass.ds(g * TPG + k, 1)], in1=upto[:], op0=ALU.is_equal, op1=ALU.mult,
                            accum_out=rank[:, b, k:k + 1])
                    ins.then_inc(rank_ready, 1)
                    dve.wait_ge(rank_ready, (g * 2 + 1) + START)
                    nc.vector.scalar_tensor_tensor(out=pick[:, b, :], in0=rank[:, b, :], scalar=1.0,
                                                   in1=src_t[:, bass.ds(g * TPG, TPG)], op0=ALU.is_equal,
                                                   op1=ALU.mult).then_inc(rank_ready, 1)
                    dve.wait_ge(rank_ready, (g * 2 + 2) + START)
                    dve.wait_ge(groups_ended, done(g - RING + 1))
                    nc.vector.tensor_scalar(sidx[:, slot, :], pick[:, b, :], trash[:, 0:1], None, ALU.add).then_inc(same_ready, 1)

                def rest(b, g):
                    dve.wait_ge(relu_ready, done(g + 1))
                    nc.vector.tensor_tensor(rr[:, b, :, :], rr[:, b, :, :], r_hi[:, b, :, 0:D], ALU.subtract).then_inc(rest_ready, 1)

                def low(b, g):
                    dve.wait_ge(mid_ready, done(g + 1))
                    nc.vector.tensor_tensor(r_lo[:, b, :, :], rr[:, b, :, :], r_mid[:, b, :, :], ALU.subtract).then_inc(parts_ready, 1)

                def add(slot, turn, g):
                    b = slot % 2
                    dve.wait_ge(z_ready, done(g + 1))
                    dve.wait_ge(gathered[slot], (turn + 1) * (16 * TPG))
                    z = z_ps[b][:, 0:TPG * D].rearrange("p (t d) -> p t d", d=D)
                    nc.vector.tensor_scalar(gidx[:, slot, :], dsti[:, bass.ds((g + RING) * TPG, TPG)], 1.0, None,
                                            ALU.mult).then_inc(gidx_ready, 1)
                    nc.vector.tensor_tensor(z, z, grow[:, slot, :, :], ALU.add).then_inc(zsum_ready, 1)

                fit = dve.value_load(fits_i[0:1, 0:1], min_val=0, max_val=1)

                def main(add):
                    def step(slot, turn, g):
                        ahead, nxt = (slot + 2) % RING, (slot + 1) % RING
                        one_hot(ahead, g + 2)
                        if add:
                            add(nxt, turn + (slot + 1) // RING, g + 1)
                        rest(nxt % 2, g + 1)
                        same_src(ahead, g + 2)
                        low(nxt % 2, g + 1)

                    one_hot(0, 0)
                    one_hot(1, 1)
                    same_src(0, 0)
                    same_src(1, 1)
                    if add:
                        add(0, 0, 0)
                    rest(0, 0)
                    low(0, 0)
                    main_loop(dve, step)

                with dve.If(fit == 1):
                    main(None)
                with dve.Else():
                    dve.wait_ge(dst_in, 16)
                    nc.vector.tensor_copy(gidx[:].rearrange("p r t -> p (r t)"), dsti[:, 0:RING * TPG]).then_inc(gidx_ready, 1)
                    main(add)
                total = tab[0][:].rearrange("p (t w) -> p t w", w=W)

                def add_table(k, b, m):
                    part = bass.ds(m * (TPG * W), TPG * W)
                    if k == 1:
                        dve.wait_ge(tables_in, done(m + 1))
                    if k == 2:
                        dve.wait_ge(added_1, done(m + 1))
                    if k == 3:
                        dve.wait_ge(added_2, done(m + 1))
                        dve.wait_ge(pool_sum, done(m * 2 + 2))
                    nc.vector.tensor_tensor(tab[0][:, part], tab[0][:, part], tab[k][:, part], ALU.add
                                            ).then_inc((added_1, added_2, added_3)[k - 1], 1)

                def counts(b, m):
                    dve.wait_ge(added_3, done(m + 1))
                    nc.vector.tensor_scalar(of(m, 1), total[:, bass.ds(m * TPG, TPG), D], 1.0, None,
                                            ALU.max).then_inc(counts_ready, 1)

                def inverse(b, m):
                    dve.wait_ge(counts_ready, done(m + 1))
                    nc.vector.reciprocal(of(m, 2), of(m, 1)).then_inc(inverse_ready, 1)

                def mean_of(b, m):
                    dve.wait_ge(inverse_ready, done(m + 1))
                    dve.wait_ge(at_raw, done(m - 1))
                    rcount = of(m, 2).rearrange("p (t a) -> p t a", a=1).to_broadcast([P, TPG, W])
                    nc.vector.tensor_tensor(a_st[:, b, :, :], total[:, bass.ds(m * TPG, TPG), :], rcount,
                                            ALU.mult).then_inc(a_ready, 1)

                def hidden_sum(b, m):
                    dve.wait_ge(hid_raw, done(m + 1))
                    dve.wait_ge(res_raw, done(m - 1))
                    nc.vector.tensor_tensor(hid_st[0:D, b, :], z_ps[b][0:D, :], ht[0:D, bass.ds(m * GE, GE)],
                                            ALU.add).then_inc(hsum_ready, 1)

                def result(b, m):
                    dve.wait_ge(res_raw, done(m + 1))
                    nc.vector.tensor_tensor(xc[:, bass.ds(m * TPG, TPG), :],
                                            c_ps[b][:, 0:TPG * D].rearrange("p (t d) -> p t d", d=D),
                                            xs[:, bass.ds(m * TPG, TPG), :], ALU.add).then_inc(res_ready, 1)

                dve.wait_ge(u_ready, done(NTURNS))
                pipelined(dve, [(4, partial(add_table, 1)), (3, partial(add_table, 3)), (1, hidden_sum), (3, counts),
                                (4, partial(add_table, 2)), (3, inverse), (0, result), (3, mean_of)])

            @block.tensor
            def _(pe):
                for s in (ht_raw, p_raw, ids_ready, z_ready, comb_ready, at_raw, hid_raw, res_raw, u_raw):
                    pe.sem_inc(s, START)
                pe.wait_ge(consts_ready, 12)
                pe.wait_ge(ones_ready, 4)

                def transposes(b, m):
                    pe.wait_ge(h_ready, done(m + 1))
                    pe.wait_ge(ht_kept, done(m - 1))
                    pe.sem_inc(pe_past, 1)
                    for k in range(TPG):
                        t = nc.tensor.transpose(srcs_ps[b][0:D, k * P:(k + 1) * P], h_st[:, b, k, :], ident[:])
                    t.then_inc(ht_raw, 1)

                def p_rows(b, m):
                    pe.wait_ge(ht_ready, done(m + 1))
                    pe.wait_ge(p_ready, done(m - 1))
                    for k in range(TPG):
                        t = nc.tensor.matmul(z_ps[b][:, k * D:(k + 1) * D], ht_st[:, b, k * P:(k + 1) * P],
                                             wts[0:W, C_W1A_TOP:C_W1A_TOP + D], start=True, stop=True)
                    t.then_inc(p_raw, 1)

                pe.wait_ge(w_in, 16)
                pe.wait_ge(wides_ready, 1)
                nc.tensor.matmul(c_ps[1][:, 0:1], ones[:], wides[:], start=True, stop=True).then_inc(fits_raw, 1)
                pipelined(pe, [(1, transposes), (0, p_rows)])
                nc.tensor.matmul(c_ps[0][0:W, 0:D], wts[0:D, C_W1B_T:C_W1B_T + W], wts[0:D, C_W2A_BOT:C_W2A_BOT + D],
                                 start=True, stop=True).then_inc(wc_raw, 1)
                pe.wait_ge(wc_ready, 2)
                pe.wait_ge(flag_ready, 1)
                pe.wait_ge(p_ready, done(NTURNS))
                pe.wait_ge(ht_kept, done(NTURNS))

                def ids(slot, turn, g):
                    b = slot % 2
                    pe.wait_ge(dig_in[slot], (turn + 1) * 16)
                    pe.wait_ge(onehot_ready, done(g))
                    pe.wait_ge(same_ready, done(g - 1))
                    nc.tensor.matmul(dsts_ps[:], spread[:, 1, :], dig[:, slot, :], start=True, stop=True)
                    nc.tensor.matmul(srcs_ps[b][:], spread[:, 0, :], dig[:, slot, :], start=True, stop=True).then_inc(ids_ready, 1)

                def z(slot, turn, g):
                    b = slot % 2
                    pe.wait_ge(et_in[slot], (turn + 1) * 16)
                    pe.wait_ge(wp_in[slot], (turn + 1) * 16)
                    pe.wait_ge(relu_ready, done(g - 1))
                    pe.wait_ge(onehot_ready, done(g + 1))
                    for k in range(TPG):
                        t = nc.tensor.matmul(z_ps[b][:, k * D:(k + 1) * D], et[:, slot, k * P:(k + 1) * P], wp[:, slot, :],
                                             start=True, stop=True)
                    t.then_inc(z_ready, 1)

                def combine(slot, g):
                    b = slot % 2
                    pe.wait_ge(same_ready, done(g + 1))
                    pe.wait_ge(parts_ready, done(g + 1))
                    pe.wait_ge(rows_ready, done(g - 1))
                    for k in range(TPG):
                        nc.tensor.matmul(c_ps[b][:, k * W:(k + 1) * W], same[:, b, k, :], r_hi[:, b, k, :],
                                         start=True, stop=False)
                        nc.tensor.matmul(c_ps[b][:, k * W:k * W + D], same[:, b, k, :], r_mid[:, b, k, :],
                                         start=False, stop=False)
                        t = nc.tensor.matmul(c_ps[b][:, k * W:k * W + D], same[:, b, k, :], r_lo[:, b, k, :],
                                             start=False, stop=True)
                    t.then_inc(comb_ready, 1)

                ids(0, 0, 0)
                ids(1, 0, 1)
                z(0, 0, 0)

                def group(slot, turn, g):
                    ids((slot + 2) % RING, turn + (slot + 2) // RING, g + 2)
                    z((slot + 1) % RING, turn + (slot + 1) // RING, g + 1)
                    combine(slot, g)

                def u(i):
                    pe.wait_ge(u_ready, done(i))
                    nc.tensor.matmul(u_ps[0:D, :], wts[0:W, C_W2A_TOP:C_W2A_TOP + D], ht[:, bass.ds(i * GE, GE)],
                                     start=True, stop=True).then_inc(u_raw, 1)

                pe.wait_ge(ht_ones, 1)
                main_loop(pe, group, u)
                pe.wait_ge(relu_ready, done(GROUPS + 1))
                pe.wait_ge(same_ready, done(GROUPS + 2))
                pe.wait_ge(rows_ready, done(GROUPS))

                def mean_t(b, m):
                    pe.wait_ge(a_ready, done(m + 1))
                    pe.wait_ge(at_ready, done(m - 1))
                    pe.sem_inc(pe_past, 1)
                    for k in range(TPG):
                        t = nc.tensor.transpose(srcs_ps[b][0:W, k * P:(k + 1) * P], a_st[:, b, k, :], ident[:])
                    t.then_inc(at_raw, 1)

                def hidden(b, m):
                    pe.wait_ge(at_ready, done(m + 1))
                    pe.wait_ge(hsum_ready, done(m - 1))
                    nc.tensor.matmul(z_ps[b][0:D, :], wc[:], at_st[:, b, :], start=True, stop=True).then_inc(hid_raw, 1)

                def out_rows(b, m):
                    pe.wait_ge(hid_ready, done(m + 1))
                    pe.wait_ge(res_ready, done(m - 1))
                    for k in range(TPG):
                        t = nc.tensor.matmul(c_ps[b][:, k * D:(k + 1) * D], hid_st[:, b, k * P:(k + 1) * P],
                                             wts[0:W, C_W2B:C_W2B + D], start=True, stop=True)
                    t.then_inc(res_raw, 1)

                pipelined(pe, [(1, hidden), (2, mean_t), (0, out_rows)])


def kernel(x, src, dst, edge_attr_64, L0_gnn_u, L0_gnn_W1a, L0_gnn_b1a, L0_gnn_W1b, L0_gnn_b1b, L0_gnn_W2a, L0_gnn_b2a,
           L0_gnn_W2b, L0_gnn_b2b):
    import numpy as np
    import concourse.bacc as bacc
    from concourse.bass_utils import run_bass_kernel_spmd

    more = EDGES - N_EDGES
    e_t = np.pad(np.asarray(edge_attr_64), ((0, more), (0, 0))).T
    src_p = np.pad(np.asarray(src), (0, more), constant_values=PAD_NODE)
    dst_p = np.pad(np.asarray(dst), (0, more), mode="edge")
    w1a, w1b, w2a, w2b = (np.asarray(w) for w in (L0_gnn_W1a, L0_gnn_W1b, L0_gnn_W2a, L0_gnn_W2b))
    b1a, b1b, b2a, b2b = (np.asarray(b)[None] for b in (L0_gnn_b1a, L0_gnn_b1b, L0_gnn_b2a, L0_gnn_b2b))
    parts = [np.concatenate([w1a[:D], b1a])] + [w1a[D:]] + [np.concatenate([w1b, b1b]).T, np.concatenate([w2a[:D], b2a]), w2a[D:],
                                                                  np.concatenate([w2b, b2b])]
    arrays = {
        "x": np.pad(np.asarray(x), ((0, NODES - N_NODES), (0, 0))),
        "e_t": e_t,
        "src_col": src_p.reshape(COLS, P).T, "dst_col": dst_p.reshape(COLS, P).T,
        "src_row": src_p.reshape(ROWP, ROWG * GE), "dst_row": dst_p.reshape(ROWP, ROWG * GE),
        "weights": np.concatenate([np.pad(p, ((0, P - len(p)), (0, 0))) for p in parts], axis=1),
    }
    arrays = {"in_" + n: np.ascontiguousarray(a) for n, a in arrays.items()}
    nc = bacc.Bacc("TRN2", target_bir_lowering=False, num_devices=1)
    args = [nc.dram_tensor(n, a.shape, mybir.dt.from_np(a.dtype), kind="ExternalInput").ap() for n, a in arrays.items()]
    out = nc.dram_tensor("out_0", (N_NODES, D), mybir.dt.float32, kind="ExternalOutput").ap()
    gnn_kernel(nc, *args, out)
    r = run_bass_kernel_spmd(nc, [arrays], core_ids=[0])
    return r.results[0]["out_0"]
```

```python
import concourse.bass as bass
from concourse import mybir
from contextlib import ExitStack
from functools import partial

N_NODES, D, N_EDGES = 6250, 64, 200000
P = 128
TPG = 4
GE = P * TPG
RING = 6
GROUPS = -(-N_EDGES // GE)
TURNS = GROUPS // RING
LEFT = GROUPS % RING
ROWG = 4
ROWP = -(-(GROUPS + RING) // ROWG)
ALL = ROWP * ROWG
EDGES = ALL * GE
COLS = EDGES // P
NT = -(-N_NODES // P)
NT += -NT % TPG
NTURNS = NT // TPG
NODES = NT * P
W = D + 1
PAD_NODE = N_NODES
TRASH = N_NODES + 1
TABLES = 6
EARLY = 3
LAG = -(-TABLES // TPG)
WIN = P - D
START = RING + 1
EPS = 1e-5

C_W1A_BOT = 0
C_W1A_TOP = C_W1A_BOT + D
C_W1B_T = C_W1A_TOP + 2 * D
C_W2A_TOP = C_W1B_T + 2 * D
C_W2A_BOT = C_W2A_TOP + 2 * D
C_W2B = C_W2A_BOT + 2 * D
C_B1B = C_W2B + 2 * D
C_B2A = C_B1B + 1
WCOLS = C_B2A + 1
PAIRS = TPG // 2
HALF = PAIRS * P

X_PARTS = [(0, 4), (4, NTURNS)]
P_PARTS = [(0, 6), (6, NTURNS - 2), (NTURNS - 2, NTURNS)]
CHUNKS = [(0, 1), (1, 3), (3, 6), (6, 9), (9, NTURNS)]
OUT_PARTS = [(0, 8), (8, NTURNS - 1), (NTURNS - 1, NTURNS)]


def done(n):
    return n + START


def gnn_kernel(nc, x, e_t, src_col, dst_col, src_row, dst_row, weights, row_biases, out):
    f32, i32, u8, bf16 = mybir.dt.float32, mybir.dt.int32, mybir.dt.uint8, mybir.dt.bfloat16
    ALU, ACT, AX = mybir.AluOpType, mybir.ActivationFunctionType, mybir.AxisListType
    assert TRASH + P <= NODES and RING * TPG % TABLES == 0 and RING % 2 == 0 and 2 * D == P

    with ExitStack() as ctx:
        def sb(name, shape, dt=f32):
            return ctx.enter_context(nc.sbuf_tensor(name, shape, dt))

        def pb(name, shape, dt=f32):
            return ctx.enter_context(nc.psum_tensor(name, shape, dt))

        def sem(name):
            return ctx.enter_context(nc.semaphore(name))

        def sems(names):
            return [sem(name) for name in names.split()]

        p_table = nc.dram_tensor("p_table", [NODES, D], f32).ap()
        digits = nc.dram_tensor("digits", [4, EDGES], bf16).ap()
        bases = nc.dram_tensor("bases", [1, ALL], i32).ap()
        sums = [nc.dram_tensor(f"sums{k}", [NODES, W], f32).ap() for k in range(TABLES)]

        ident = sb("ident", [P, P])
        upto = sb("upto", [P, P])
        spread = sb("spread", [4, 2, P], bf16)
        wts = sb("wts", [P, WCOLS])
        wcq = sb("wcq", [P, P + 1])
        rowb = sb("rowb", [P, 2, D])
        ident_b = sb("ident_b", [P, P], bf16)
        trash_i = sb("trash_i", [P, 1], i32)
        trash = sb("trash", [P, 1])
        untrash = sb("untrash", [P, 1])
        epsb = sb("epsb", [P, 1])
        first_root = sb("first_root", [P, 1])
        ones = sb("ones", [ROWP, P])

        xs = sb("xs", [P, NT, D])
        xc = sb("xc", [P, NT, D])
        stat = sb("stat", [P, 3, NT])
        h_st = sb("h_st", [P, 2, TPG, D])
        ht_st = sb("ht_st", [P, 2, HALF])
        ht = sb("ht", [P, NTURNS * HALF])
        tab = [sb(f"tab{k}", [P, NT * W]) for k in range(TABLES)]
        a_st = sb("a_st", [P, 2, TPG, D])
        at_st = sb("at_st", [P, 2, HALF])
        met = sb("met", [P, 2, TPG, D], bf16)
        hid_st = sb("hid_st", [P, 2, HALF])
        sq = tab[5][:, 0:NT * D].rearrange("p (t d) -> p t d", d=D)

        total = tab[0][:].rearrange("p (t w) -> p t w", w=W)

        srcf = sb("srcf", [P, COLS])
        src_t = sb("src_t", [P, COLS])
        dsti = tab[5][:, 0:COLS].bitcast(i32)
        basew = sb("basew", [P, ALL])
        base_i = sb("base_i", [P, ALL], i32)
        wlane_i = sb("wlane_i", [P, 1], i32)
        wlane = sb("wlane", [P, 1])
        glow = sb("glow", [ROWP, 2, ROWG])
        glow_i = sb("glow_i", [ROWP, ROWG], i32)
        wide = sb("wide", [ROWP, ROWG])
        wides = sb("wides", [ROWP, 1])
        fits = sb("fits", [P, 1])
        fits_i = sb("fits_i", [P, 1], i32)
        ids_i = src_t[:].bitcast(i32)
        row_i = [tab[1 + r][0:ROWP, 0:ROWG * GE].bitcast(i32) for r in range(2)]
        row_bytes = [tab[1 + r][0:ROWP, 0:ROWG * GE].bitcast(u8).rearrange("p (c b) -> p b c", b=4)[:, 0:2, :] for r in range(2)]
        row_d = [tab[3 + r][0:ROWP, 0:ROWG * GE].bitcast(bf16).rearrange("p (d c) -> p d c", d=2) for r in range(2)]

        et = sb("et", [P, RING, GE])
        wp = sb("wp", [P, RING, D])
        dig = sb("dig", [4, RING, GE], bf16)
        gidx = sb("gidx", [P, RING, TPG], i32)
        grow = sb("grow", [P, RING, TPG, D])
        same = sb("same", [P, 2, TPG, P], bf16)
        rank = sb("rank", [P, 2, TPG])
        pick = sb("pick", [P, 2, TPG])
        sidx = sb("sidx", [P, RING, TPG], i32)
        rr = sb("rr", [P, 2, TPG, D])
        r_hi = sb("r_hi", [P, 2, TPG, W], bf16)
        r_mid = sb("r_mid", [P, 2, TPG, D], bf16)
        r_lo = sb("r_lo", [P, 2, TPG, D], bf16)
        vv = sb("vv", [P, RING, TPG, W])

        srcs_ps = [pb(f"srcs_ps{b}", [P, 512]) for b in range(2)]
        dsts_ps = pb("dsts_ps", [P, 512])
        u_ps = pb("u_ps", [P, 512])
        met_ps = [dsts_ps, u_ps]
        z_ps = [pb(f"z_ps{b}", [P, 512]) for b in range(2)]
        c_ps = [pb(f"c_ps{b}", [P, 512]) for b in range(2)]

        x_in = [sem(f"x_in{k}") for k in range(len(X_PARTS))]
        sums_in = [sem(f"sums_in{c}") for c in range(len(CHUNKS))]
        rows_in = [sem(f"rows_in{r}") for r in range(2)]
        w_in, rowb_in, src_in, dst_in, base_in = sems("w_in rowb_in src_in dst_in base_in")
        digits_out, bases_out, ptab_out, res_out = sems("digits_out bases_out ptab_out res_out")
        et_in, wp_in, dig_in, gathered = ([sem(f"{n}{s}") for s in range(RING)] for n in ("et_in", "wp_in", "dig_in", "gathered"))
        scattered = [sem(f"scattered{k}") for k in range(TABLES)]
        zeros_ready, consts_ready, ones_ready, ident_b_ready = sems("zeros_ready consts_ready ones_ready ident_b_ready")
        digits_ready = [sem(f"digits_ready{r}") for r in range(2)]
        src_ready, bases_ready, wides_ready, fits_raw, flag_ready = sems("src_ready bases_ready wides_ready fits_raw flag_ready")
        wc_raw, wc_ready, dve_step = sems("wc_raw wc_ready dve_step")
        pool_past, pe_past = sems("pool_past pe_past")
        sum_ready, xc_ready, sq_ready, var_ready = sems("sum_ready xc_ready sq_ready var_ready")
        std_ready, rstd_ready, h_ready = sems("std_ready rstd_ready h_ready")
        ht_raw, ht_ready, ht_kept, p_raw, p_ready, u_raw, u_ready = sems("ht_raw ht_ready ht_kept p_raw p_ready u_raw u_ready")
        ids_ready, onehot_ready, rank_ready, same_ready = sems("ids_ready onehot_ready rank_ready same_ready")
        z_ready, zsum_ready, gidx_ready, relu_ready = sems("z_ready zsum_ready gidx_ready relu_ready")
        rest_ready, mid_ready, parts_ready = sems("rest_ready mid_ready parts_ready")
        comb_ready, rows_ready, groups_ended = sems("comb_ready rows_ready groups_ended")
        tables_in, added_1, pool_sum, added_3, xb_ready = sems("tables_in added_1 pool_sum added_3 xb_ready")
        counts_ready, inverse_ready, a_ready, at_raw, at_ready = sems("counts_ready inverse_ready a_ready at_raw at_ready")
        met_ready, met_raw, ustar_ready = sems("met_ready met_raw ustar_ready")
        hid_raw, hsum_ready, hid_ready, res_raw, res_ready = sems("hid_raw hsum_ready hid_ready res_raw res_ready")

        def ended(t):
            return 16 * (1 + len(range(t, GROUPS * TPG, TABLES)))

        def main_loop(eng, step, beside=None):
            def turns(first, last, beside):
                with eng.Fori(first, last) as i:
                    for s in range(RING):
                        step(s, i, i * RING + s)
                    if beside:
                        beside(i)

            if beside:
                turns(0, NTURNS, beside)
            turns(NTURNS if beside else 0, TURNS, None)
            for s in range(LEFT):
                step(s, TURNS, TURNS * RING + s)

        def pipelined(eng, stages):
            far = max(lead for lead, _ in stages)

            def step(b, t, peeled=False):
                for lead, stage in stages:
                    if not peeled or 0 <= t + lead < NTURNS:
                        stage((b + lead) % 2, t + lead)

            for t in range(-far, 0):
                step(t % 2, t, peeled=True)
            pairs = (NTURNS - far) // 2
            with eng.Fori(0, pairs) as i:
                for b in range(2):
                    step(b, i * 2 + b)
            for t in range(2 * pairs, NTURNS):
                step(t % 2, t, peeled=True)

        with nc.Block() as block:

            @block.sync
            def _(sp):
                x_rows = x.rearrange("(p t) d -> p t d", t=NT)
                sp.dma_start(row_i[0], dst_row).then_inc(rows_in[0], 16)
                for k, (m, n) in enumerate(X_PARTS):
                    sp.dma_start(xs[:, m * TPG:n * TPG, :], x_rows[:, m * TPG:n * TPG, :]).then_inc(x_in[k], 16)
                    if k == 0:
                        sp.dma_start(wts[:], weights).then_inc(w_in, 16)
                        sp.dma_start(rowb[:].rearrange("p b d -> p (b d)"), row_biases.to_broadcast([P, 2 * D])
                                     ).then_inc(rowb_in, 16)
                        sp.dma_start(row_i[1], src_row).then_inc(rows_in[1], 16)
                sp.wait_ge(bases_ready, 1)
                sp.dma_start(bases.rearrange("a (p r) -> (a p) r", r=ROWG), glow_i[:]).then_inc(bases_out, 16)
                sp.dma_start(ids_i, src_col).then_inc(src_in, 16)
                sp.wait_ge(bases_out, 16)
                sp.dma_start(base_i[:], bases.to_broadcast([P, ALL])).then_inc(base_in, 16)
                for s in range(RING):
                    sp.dma_start(et[0:D, s, :], e_t[:, s * GE:(s + 1) * GE]).then_inc(et_in[s], 16)
                table = p_table.rearrange("(p t) d -> p t d", t=NT)

                def store_p(m, n):
                    sp.wait_ge(p_ready, done(n))
                    sp.dma_start(table[:, m * TPG:n * TPG, :], xc[:, m * TPG:n * TPG, :]).then_inc(ptab_out, 16)

                def load_digits(slot, g):
                    sp.dma_start(dig[:, slot, :], digits[:, bass.ds(g * GE, GE)]).then_inc(dig_in[slot], 16)

                def window(g):
                    return sp.value_load(base_i[0:1, bass.ds(g, 1)], min_val=0, max_val=N_NODES - 1)

                def load_window(slot, base):
                    sp.dma_start(wp[D:P, slot, :], p_table[bass.ds(base, WIN), :]).then_inc(wp_in[slot], 16)

                sp.wait_ge(base_in, 16)
                first = [window(s) for s in range(RING)]
                store_p(*P_PARTS[0])
                for r, at in enumerate((2, 0)):
                    sp.wait_ge(digits_ready[r], 1)
                    sp.dma_start(digits[at:at + 2].rearrange("d (p c) -> p d c", p=ROWP), row_d[r]).then_inc(digits_out, 16)
                store_p(*P_PARTS[1])
                store_p(*P_PARTS[2])
                sp.wait_ge(digits_out, 32)
                for s in range(RING):
                    load_digits(s, s)
                sp.wait_ge(ptab_out, 16 * len(P_PARTS))
                for s in range(RING):
                    load_window(s, first[s])
                with sp.Fori(0, TURNS) as i:
                    for s in range(RING):
                        g = i * RING + s
                        sp.wait_ge(z_ready, done(g + 1))
                        load_digits(s, g + RING)
                        load_window(s, window(g + RING))
                        sp.dma_start(et[0:D, s, :], e_t[:, bass.ds((g + RING) * GE, GE)]).then_inc(et_in[s], 16)
                for s in range(RING):
                    for ring in (et_in, wp_in, dig_in):
                        sp.wait_ge(ring[s], 16 * (TURNS + 1))
                sp.wait_ge(relu_ready, done(GROUPS + 1))
                for t in range(TABLES):
                    sp.wait_ge(scattered[t], ended(t))
                def load_sums(c, m, n):
                    for t in range(TABLES):
                        sp.dma_start(tab[t][:, m * TPG * W:n * TPG * W],
                                     sums[t].rearrange("(p t) w -> p (t w)", t=NT)[:, m * TPG * W:n * TPG * W]
                                     ).then_inc(sums_in[c], 16)

                sp.sem_inc(tables_in, START)
                load_sums(0, *CHUNKS[0])
                for c, (m, n) in enumerate(CHUNKS):
                    if c + 1 < len(CHUNKS):
                        load_sums(c + 1, *CHUNKS[c + 1])
                    sp.wait_ge(sums_in[c], 16 * TABLES)
                    sp.sem_inc(tables_in, n - m)
                full = N_NODES // NT
                rest = N_NODES - full * NT
                rows = out[0:full * NT, :].rearrange("(p t) d -> p t d", t=NT)
                for m, n in OUT_PARTS:
                    sp.wait_ge(res_ready, done(n))
                    sp.dma_start(rows[:, m * TPG:n * TPG, :], xc[0:full, m * TPG:n * TPG, :]).then_inc(res_out, 16)
                    if m == 0:
                        sp.dma_start(out[full * NT:, :].rearrange("(p t) d -> p t d", t=rest),
                                     xc[full:full + 1, 0:rest, :]).then_inc(res_out, 16)
                sp.wait_ge(res_out, 16 * (len(OUT_PARTS) + 1))

            @block.gpsimd
            def _(pool):
                nc.gpsimd.memset(ident[:], 0.0).then_inc(consts_ready, 1)
                nc.gpsimd.memset(upto[:], 1.0).then_inc(consts_ready, 1)
                nc.gpsimd.iota(trash_i[:], pattern=[[0, 1]], base=TRASH, channel_multiplier=1).then_inc(consts_ready, 1)
                nc.gpsimd.iota(wlane_i[:], pattern=[[0, 1]], base=1 - D, channel_multiplier=1).then_inc(consts_ready, 1)
                nc.gpsimd.memset(spread[:], 0.0).then_inc(consts_ready, 1)
                pool.wait_ge(consts_ready, 5)
                nc.gpsimd.affine_select(out=ident[:], in_=ident[:], compare_op=ALU.not_equal, fill=1.0, base=0,
                                        pattern=[[-1, P]], channel_multiplier=1).then_inc(consts_ready, 1)
                nc.gpsimd.affine_select(out=upto[:], in_=upto[:], compare_op=ALU.is_ge, fill=0.0, base=0,
                                        pattern=[[-1, P]], channel_multiplier=1).then_inc(consts_ready, 1)
                nc.gpsimd.affine_select(out=spread[:], in_=spread[:], compare_op=ALU.not_equal, fill=1.0, base=0,
                                        pattern=[[-2, 2], [0, P]], channel_multiplier=1).then_inc(consts_ready, 1)
                pool.wait_ge(consts_ready, 8)
                nc.gpsimd.affine_select(out=spread[:], in_=spread[:], compare_op=ALU.not_equal, fill=256.0, base=-1,
                                        pattern=[[-2, 2], [0, P]], channel_multiplier=1).then_inc(consts_ready, 1)
                nc.gpsimd.tensor_copy(trash[:], trash_i[:]).then_inc(consts_ready, 1)
                nc.gpsimd.tensor_copy(wlane[:], wlane_i[:]).then_inc(consts_ready, 1)
                pool.wait_ge(consts_ready, 11)
                nc.gpsimd.tensor_scalar(untrash[:], trash[:], -1.0, None, ALU.mult).then_inc(consts_ready, 1)

                def zero(k):
                    pool.dma_start(sums[k].rearrange("(p t) w -> p (t w)", t=NT), tab[0][:]).then_inc(scattered[k], 16)

                nc.gpsimd.memset(tab[0][:], 0.0).then_inc(zeros_ready, 1)
                pool.wait_ge(zeros_ready, 1)
                for part in x_in:
                    pool.wait_ge(part, 16)
                for k in range(EARLY):
                    zero(k)
                pool.wait_ge(consts_ready, 12)
                pool.wait_ge(rows_in[1], 16)
                nc.gpsimd.tensor_copy(row_d[1], row_bytes[1]).then_inc(digits_ready[1], 1)

                def gather(slot):
                    for k in range(TPG):
                        nc.gpsimd.indirect_dma_start(
                            out=grow[:, slot, k, :], out_offset=None, in_=p_table[:, :],
                            in_offset=bass.IndirectOffsetOnAxis(ap=gidx[:, slot, k:k + 1], axis=0),
                        ).then_inc(gathered[slot], 16)

                def scatter(slot, turn, g):
                    for k in range(TPG):
                        before, t = divmod(slot * TPG + k, TABLES)
                        if k == 0:
                            pool.wait_ge(same_ready, done(g + 1))
                            pool.wait_ge(rows_ready, done(g + 1))
                        pool.wait_ge(scattered[t], (turn * (RING * TPG // TABLES) + before + 1) * 16)
                        pool.sem_inc(pool_past, 1)
                        nc.gpsimd.indirect_dma_start(
                            out=sums[t][:, :],
                            out_offset=bass.IndirectOffsetOnAxis(ap=sidx[:, slot, k:k + 1], axis=0),
                            in_=vv[:, slot, k, :], in_offset=None, compute_op=ALU.add,
                        ).then_inc(scattered[t], 16)
                    pool.sem_inc(groups_ended, 1)

                pool.sem_inc(groups_ended, START - LAG)
                pool.wait_ge(p_ready, done(NTURNS))
                zero(EARLY)
                pool.wait_ge(wp_in[0], 16)
                for k in range(EARLY + 1, TABLES):
                    zero(k)
                pool.wait_ge(flag_ready, 1)
                fit = pool.value_load(fits_i[0:1, 0:1], min_val=0, max_val=1)
                with pool.If(fit == 1):
                    main_loop(pool, scatter)
                with pool.Else():
                    pool.dma_start(dsti, dst_col).then_inc(dst_in, 16)
                    pool.wait_ge(ptab_out, 16 * len(P_PARTS))
                    pool.wait_ge(gidx_ready, done(1))
                    for s in range(RING - 1):
                        gather(s)

                    def both(slot, turn, g):
                        pool.wait_ge(gidx_ready, done(g + 1))
                        pool.wait_ge(zsum_ready, done(g))
                        pool.sem_inc(pool_past, 1)
                        gather((slot + RING - 1) % RING)
                        scatter(slot, turn, g)

                    main_loop(pool, both)
                    for s in range(RING):
                        pool.wait_ge(gathered[s], 16 * TPG * len(range(s, GROUPS + RING - 1, RING)))
                pool.wait_ge(rowb_in, 16)
                b2b = rowb[:, 1:2, :].to_broadcast([P, NT, D])
                nc.gpsimd.tensor_tensor(xs[:], xs[:], b2b, ALU.add).then_inc(xb_ready, 1)
                pool.sem_inc(pool_sum, START)
                with pool.Fori(0, NTURNS) as m:
                    part = bass.ds(m * (TPG * W), TPG * W)
                    pool.wait_ge(tables_in, done(m + 1))
                    for k, t in enumerate((2, 4, 5)):
                        if k > 0:
                            pool.wait_ge(pool_sum, done(m * 3 + k))
                        nc.gpsimd.tensor_tensor(tab[3][:, part], tab[3][:, part], tab[t][:, part], ALU.add).then_inc(pool_sum, 1)

            @block.scalar
            def _(act):
                for s in (sq_ready, std_ready, ht_ready, ht_kept, relu_ready, mid_ready, rows_ready, u_ready, met_ready, at_ready,
                          hid_ready):
                    act.sem_inc(s, START)
                act.wait_ge(rows_in[0], 16)
                nc.scalar.activation(row_d[0], row_bytes[0], ACT.Copy).then_inc(digits_ready[0], 1)
                act.wait_ge(ones_ready, 3)
                nc.scalar.activation(first_root[:], epsb[:], ACT.Sqrt)

                def square(b, m):
                    act.wait_ge(xc_ready, done(m + 1))
                    nc.scalar.activation(sq[:, bass.ds(m * TPG, TPG), :], xc[:, bass.ds(m * TPG, TPG), :],
                                         ACT.Square).then_inc(sq_ready, 1)

                def root(b, m):
                    act.wait_ge(var_ready, done(m + 1))
                    nc.scalar.activation(stat[:, 2, bass.ds(m * TPG, TPG)], stat[:, 1, bass.ds(m * TPG, TPG)], ACT.Sqrt,
                                         bias=epsb[:], scale=1.0 / D).then_inc(std_ready, 1)

                def h_keep(b, m):
                    act.wait_ge(ht_raw, done(m + 1))
                    act.wait_ge(p_raw, done(m - 1))
                    nc.scalar.activation(ht_st[:, b, :], srcs_ps[b][:, 0:HALF], ACT.Relu).then_inc(ht_ready, 1)
                    nc.scalar.activation(ht[:, bass.ds(m * HALF, HALF)], srcs_ps[b][:, 0:HALF], ACT.Relu).then_inc(ht_kept, 1)

                pipelined(act, [(1, h_keep), (5, square), (4, root)])
                act.wait_ge(src_in, 16)
                nc.scalar.activation(srcf[:], ids_i, ACT.Copy).then_inc(src_ready, 1)
                act.wait_ge(src_ready, 1)
                act.wait_ge(consts_ready, 12)
                nc.scalar.activation(src_t[:], srcf[:], ACT.Identity, bias=untrash[:]).then_inc(src_ready, 1)
                act.wait_ge(w_in, 16)
                bottom = wts[0:D, C_W1A_BOT:C_W1A_BOT + D].rearrange("p (r d) -> p r d", r=1).to_broadcast([D, RING, D])
                nc.scalar.activation(wp[0:D, :, :], bottom, ACT.Copy).then_inc(wc_ready, 1)
                act.wait_ge(wc_raw, 1)
                nc.scalar.activation(wcq[:], c_ps[0][:, 0:P + 1], ACT.Copy).then_inc(wc_ready, 1)
                nc.scalar.activation(ident_b[:], ident[:], ACT.Copy).then_inc(ident_b_ready, 1)

                def main(summed):
                    def relu(b, g):
                        z = z_ps[b][:, 0:TPG * D].rearrange("p (t d) -> p t d", d=D)
                        act.wait_ge(summed, done(g + 1))
                        act.wait_ge(parts_ready, done(g - 1))
                        nc.scalar.activation(rr[:, b, :, :], z, ACT.Relu)
                        act.wait_ge(comb_ready, done(g - 1))
                        nc.scalar.activation(r_hi[:, b, :, 0:D], z, ACT.Relu).then_inc(relu_ready, 1)

                    def mid(b, g):
                        act.wait_ge(rest_ready, done(g + 1))
                        nc.scalar.activation(r_mid[:, b, :, :], rr[:, b, :, :], ACT.Copy).then_inc(mid_ready, 1)

                    def step(slot, turn, g):
                        relu((slot + 1) % 2, g + 1)
                        act.wait_ge(comb_ready, done(g + 1))
                        act.wait_ge(groups_ended, done(g - RING + 1))
                        nc.scalar.activation(vv[:, slot, :, :], c_ps[slot % 2][:, 0:TPG * W].rearrange("p (t w) -> p t w", w=W),
                                             ACT.Copy).then_inc(rows_ready, 1)
                        mid((slot + 1) % 2, g + 1)

                    def u_keep(i):
                        act.wait_ge(u_raw, done(i + 1))
                        nc.scalar.activation(ht[:, bass.ds(i * HALF, HALF)], u_ps[:, 0:HALF], ACT.Identity,
                                             bias=wts[:, C_B2A:C_B2A + 1]).then_inc(u_ready, 1)

                    relu(0, 0)
                    mid(0, 0)
                    main_loop(act, step, u_keep)

                act.wait_ge(flag_ready, 1)
                fit = act.value_load(fits_i[0:1, 0:1], min_val=0, max_val=1)
                with act.If(fit == 1):
                    main(z_ready)
                with act.Else():
                    main(zsum_ready)

                def mean_t_keep(b, m):
                    act.wait_ge(at_raw, done(m + 1))
                    act.wait_ge(hid_raw, done(m - 1))
                    nc.scalar.activation(at_st[:, b, :], srcs_ps[b][:, 0:HALF], ACT.Copy).then_inc(at_ready, 1)

                def hidden(b, m):
                    act.wait_ge(hsum_ready, done(m + 1))
                    nc.scalar.activation(hid_st[:, b, :], hid_st[:, b, :], ACT.Relu).then_inc(hid_ready, 1)

                def met_rows(b, m):
                    act.wait_ge(added_3, done(m + 1))
                    act.wait_ge(met_raw, done(m - 1))
                    count = total[:, bass.ds(m * TPG, TPG), D:W].to_broadcast([P, TPG, D])
                    nc.scalar.activation(met[:, b, :, :], count, ACT.Sign).then_inc(met_ready, 1)

                pipelined(act, [(2, mean_t_keep), (1, hidden), (3, met_rows)])

            @block.vector
            def _(dve):
                steps = [0]

                def step(ins):
                    steps[0] += 1
                    ins.then_inc(dve_step, 1)
                    dve.wait_ge(dve_step, steps[0])

                for s in (sum_ready, xc_ready, var_ready, rstd_ready, h_ready, p_ready, onehot_ready, rank_ready, same_ready,
                          zsum_ready, gidx_ready, rest_ready, parts_ready, added_1, added_3, counts_ready, inverse_ready,
                          a_ready, ustar_ready, hsum_ready, res_ready):
                    dve.sem_inc(s, START)
                nc.vector.memset(epsb[:], EPS).then_inc(ones_ready, 1)
                nc.vector.memset(ones[:], 1.0).then_inc(ones_ready, 1)
                nc.vector.memset(r_hi[:, :, :, D:W], 1.0).then_inc(ones_ready, 1)
                dve.wait_ge(rows_in[0], 16)
                by_group = row_i[0].rearrange("p (r c) -> p r c", r=ROWG)
                step(nc.vector.tensor_reduce(glow[:, 0, :], by_group, AX.X, ALU.min))
                nc.vector.tensor_copy(glow_i[:], glow[:, 0, :]).then_inc(bases_ready, 1)

                def of(m, k):
                    return stat[:, k, bass.ds(m * TPG, TPG)]

                def on_rows(m, k):
                    return of(m, k).rearrange("p (t a) -> p t a", a=1).to_broadcast([P, TPG, D])

                def row_sum(b, m):
                    for part, (first, _) in zip(x_in, X_PARTS):
                        if isinstance(m, int) and m == first:
                            dve.wait_ge(part, 16)
                    nc.vector.tensor_reduce(of(m, 0), xs[:, bass.ds(m * TPG, TPG), :], AX.X, ALU.add).then_inc(sum_ready, 1)

                def centre(b, m):
                    dve.wait_ge(sum_ready, done(m + 1))
                    nc.vector.scalar_tensor_tensor(out=xc[:, bass.ds(m * TPG, TPG), :], in0=on_rows(m, 0), scalar=-1.0 / D,
                                                   in1=xs[:, bass.ds(m * TPG, TPG), :], op0=ALU.mult,
                                                   op1=ALU.add).then_inc(xc_ready, 1)

                def square_sum(b, m):
                    dve.wait_ge(sq_ready, done(m + 1))
                    nc.vector.tensor_reduce(of(m, 1), sq[:, bass.ds(m * TPG, TPG), :], AX.X, ALU.add).then_inc(var_ready, 1)

                def rstd(b, m):
                    dve.wait_ge(std_ready, done(m + 1))
                    nc.vector.reciprocal(of(m, 0), of(m, 2)).then_inc(rstd_ready, 1)

                def norm(b, m):
                    dve.wait_ge(rstd_ready, done(m + 1))
                    dve.wait_ge(ht_raw, done(m - 1))
                    nc.vector.tensor_tensor(h_st[:, b, :, :], xc[:, bass.ds(m * TPG, TPG), :], on_rows(m, 0),
                                            ALU.mult).then_inc(h_ready, 1)

                def p_keep(b, m):
                    dve.wait_ge(p_raw, done(m + 1))
                    nc.vector.tensor_tensor(xc[:, bass.ds(m * TPG, TPG), :],
                                            z_ps[b][:, 0:TPG * D].rearrange("p (t d) -> p t d", d=D),
                                            rowb[:, 0:1, :].to_broadcast([P, TPG, D]), ALU.add).then_inc(p_ready, 1)

                dve.wait_ge(rowb_in, 16)
                pipelined(dve, [(2, norm), (3, rstd), (4, square_sum), (5, centre), (6, row_sum), (0, p_keep)])
                step(nc.vector.tensor_reduce(glow[:, 1, :], by_group, AX.X, ALU.max))
                step(nc.vector.tensor_tensor(wide[:], glow[:, 1, :], glow[:, 0, :], ALU.subtract))
                step(nc.vector.tensor_scalar(wide[:], wide[:], float(WIN - 1), None, ALU.is_gt))
                nc.vector.tensor_reduce(wides[:], wide[:], AX.X, ALU.add).then_inc(wides_ready, 1)
                dve.wait_ge(fits_raw, 1)
                step(nc.vector.tensor_scalar(fits[:], c_ps[1][:, 0:1], 0.0, None, ALU.is_equal))
                nc.vector.tensor_copy(fits_i[:], fits[:]).then_inc(flag_ready, 1)
                dve.wait_ge(consts_ready, 12)
                dve.wait_ge(base_in, 16)
                step(nc.vector.tensor_copy(basew[:], base_i[:]))
                step(nc.vector.tensor_scalar(basew[:], basew[:], wlane[:, 0:1], fits[:, 0:1], ALU.add, ALU.mult))
                step(nc.vector.tensor_scalar(basew[:], basew[:], 1.0, None, ALU.subtract))
                dve.wait_ge(src_ready, 2)

                def one_hot(slot, g):
                    dve.wait_ge(ids_ready, done(g + 1))
                    dve.wait_ge(z_ready, done(g - RING + 1))
                    nc.vector.tensor_scalar(et[D:P, slot, :], dsts_ps[D:P, :], basew[D:P, bass.ds(g, 1)], None,
                                            ALU.is_equal).then_inc(onehot_ready, 1)

                def same_src(slot, g):
                    b = slot % 2
                    dve.wait_ge(comb_ready, done(g - 1))
                    for k in range(TPG):
                        ins = nc.vector.scalar_tensor_tensor(
                            out=same[:, b, k, :], in0=srcs_ps[b][:, k * P:(k + 1) * P],
                            scalar=srcf[:, bass.ds(g * TPG + k, 1)], in1=upto[:], op0=ALU.is_equal, op1=ALU.mult,
                            accum_out=rank[:, b, k:k + 1])
                    ins.then_inc(rank_ready, 1)
                    dve.wait_ge(rank_ready, (g * 2 + 1) + START)
                    nc.vector.scalar_tensor_tensor(out=pick[:, b, :], in0=rank[:, b, :], scalar=1.0,
                                                   in1=src_t[:, bass.ds(g * TPG, TPG)], op0=ALU.is_equal,
                                                   op1=ALU.mult).then_inc(rank_ready, 1)
                    dve.wait_ge(rank_ready, (g * 2 + 2) + START)
                    dve.wait_ge(groups_ended, done(g - RING + 1))
                    nc.vector.tensor_scalar(sidx[:, slot, :], pick[:, b, :], trash[:, 0:1], None, ALU.add).then_inc(same_ready, 1)

                def rest(b, g):
                    dve.wait_ge(relu_ready, done(g + 1))
                    nc.vector.tensor_tensor(rr[:, b, :, :], rr[:, b, :, :], r_hi[:, b, :, 0:D], ALU.subtract).then_inc(rest_ready, 1)

                def low(b, g):
                    dve.wait_ge(mid_ready, done(g + 1))
                    nc.vector.tensor_tensor(r_lo[:, b, :, :], rr[:, b, :, :], r_mid[:, b, :, :], ALU.subtract).then_inc(parts_ready, 1)

                def add(slot, turn, g):
                    b = slot % 2
                    dve.wait_ge(z_ready, done(g + 1))
                    dve.wait_ge(gathered[slot], (turn + 1) * (16 * TPG))
                    z = z_ps[b][:, 0:TPG * D].rearrange("p (t d) -> p t d", d=D)
                    nc.vector.tensor_scalar(gidx[:, slot, :], dsti[:, bass.ds((g + RING) * TPG, TPG)], 1.0, None,
                                            ALU.mult).then_inc(gidx_ready, 1)
                    nc.vector.tensor_tensor(z, z, grow[:, slot, :, :], ALU.add).then_inc(zsum_ready, 1)

                fit = dve.value_load(fits_i[0:1, 0:1], min_val=0, max_val=1)

                def main(add):
                    def step(slot, turn, g):
                        ahead, nxt = (slot + 2) % RING, (slot + 1) % RING
                        one_hot(ahead, g + 2)
                        if add:
                            add(nxt, turn + (slot + 1) // RING, g + 1)
                        rest(nxt % 2, g + 1)
                        same_src(ahead, g + 2)
                        low(nxt % 2, g + 1)

                    one_hot(0, 0)
                    same_src(0, 0)
                    one_hot(1, 1)
                    if add:
                        add(0, 0, 0)
                    rest(0, 0)
                    low(0, 0)
                    same_src(1, 1)
                    main_loop(dve, step)

                with dve.If(fit == 1):
                    main(None)
                with dve.Else():
                    dve.wait_ge(dst_in, 16)
                    nc.vector.tensor_copy(gidx[:].rearrange("p r t -> p (r t)"), dsti[:, 0:RING * TPG]).then_inc(gidx_ready, 1)
                    main(add)

                def add_table(k, b, m):
                    part = bass.ds(m * (TPG * W), TPG * W)
                    if k == 1:
                        dve.wait_ge(tables_in, done(m + 1))
                    if k == 3:
                        dve.wait_ge(added_1, done(m + 1))
                        dve.wait_ge(pool_sum, done(m * 3 + 3))
                    nc.vector.tensor_tensor(tab[0][:, part], tab[0][:, part], tab[k][:, part], ALU.add
                                            ).then_inc(added_1 if k == 1 else added_3, 1)

                def counts(b, m):
                    dve.wait_ge(added_3, done(m + 1))
                    nc.vector.tensor_scalar(of(m, 1), total[:, bass.ds(m * TPG, TPG), D], 1.0, None,
                                            ALU.max).then_inc(counts_ready, 1)

                def inverse(b, m):
                    dve.wait_ge(counts_ready, done(m + 1))
                    nc.vector.reciprocal(of(m, 2), of(m, 1)).then_inc(inverse_ready, 1)

                def mean_of(b, m):
                    dve.wait_ge(inverse_ready, done(m + 1))
                    dve.wait_ge(at_raw, done(m - 1))
                    rcount = of(m, 2).rearrange("p (t a) -> p t a", a=1).to_broadcast([P, TPG, D])
                    nc.vector.tensor_tensor(a_st[:, b, :, :], total[:, bass.ds(m * TPG, TPG), 0:D], rcount,
                                            ALU.mult).then_inc(a_ready, 1)

                def ustar(b, m):
                    block = ht[:, bass.ds(m * HALF, HALF)]
                    dve.wait_ge(met_raw, done(m + 1))
                    nc.vector.scalar_tensor_tensor(out=block, in0=met_ps[b][:, 0:HALF], scalar=wcq[:, P:P + 1], in1=block,
                                                   op0=ALU.mult, op1=ALU.add).then_inc(ustar_ready, 1)

                def hidden_sum(b, m):
                    dve.wait_ge(hid_raw, done(m + 1))
                    dve.wait_ge(ustar_ready, done(m + 1))
                    dve.wait_ge(res_raw, done(m - 1))
                    nc.vector.tensor_tensor(hid_st[:, b, :], z_ps[b][:, 0:HALF], ht[:, bass.ds(m * HALF, HALF)],
                                            ALU.add).then_inc(hsum_ready, 1)

                def result(b, m):
                    dve.wait_ge(res_raw, done(m + 1))
                    nc.vector.tensor_tensor(xc[:, bass.ds(m * TPG, TPG), :],
                                            c_ps[b][:, 0:TPG * D].rearrange("p (t d) -> p t d", d=D),
                                            xs[:, bass.ds(m * TPG, TPG), :], ALU.add).then_inc(res_ready, 1)

                dve.wait_ge(u_ready, done(NTURNS))
                dve.wait_ge(xb_ready, 1)
                pipelined(dve, [(3, partial(add_table, 3)), (1, ustar), (3, counts), (4, partial(add_table, 1)),
                                (3, inverse), (1, hidden_sum), (3, mean_of), (0, result)])

            @block.tensor
            def _(pe):
                for s in (ht_raw, p_raw, ids_ready, z_ready, comb_ready, at_raw, hid_raw, res_raw, u_raw, met_raw):
                    pe.sem_inc(s, START)
                pe.wait_ge(consts_ready, 12)
                pe.wait_ge(ones_ready, 3)

                def pair(buffer, b, j):
                    return buffer[:, b, 2 * j:2 * j + 2, :].rearrange("p t d -> p (t d)")

                def transposes(b, m):
                    pe.wait_ge(h_ready, done(m + 1))
                    pe.wait_ge(ht_kept, done(m - 1))
                    pe.sem_inc(pe_past, 1)
                    for j in range(PAIRS):
                        t = nc.tensor.transpose(srcs_ps[b][:, j * P:(j + 1) * P], pair(h_st, b, j), ident[:])
                    t.then_inc(ht_raw, 1)

                def p_rows(b, m):
                    pe.wait_ge(ht_ready, done(m + 1))
                    pe.wait_ge(p_ready, done(m - 1))
                    for j in range(PAIRS):
                        t = nc.tensor.matmul(z_ps[b][:, j * P:(j + 1) * P], ht_st[:, b, j * P:(j + 1) * P],
                                             wts[:, C_W1A_TOP:C_W1A_TOP + P], start=True, stop=True)
                    t.then_inc(p_raw, 1)

                pe.wait_ge(w_in, 16)
                pipelined(pe, [(1, transposes), (0, p_rows)])
                pe.wait_ge(wides_ready, 1)
                nc.tensor.matmul(c_ps[1][:, 0:1], ones[:], wides[:], start=True, stop=True).then_inc(fits_raw, 1)
                nc.tensor.matmul(c_ps[0][:, 0:P], wts[:, C_W1B_T:C_W1B_T + P], wts[:, C_W2A_BOT:C_W2A_BOT + P],
                                 start=True, stop=True)
                nc.tensor.matmul(c_ps[0][:, P:P + 1], wts[:, C_W2A_BOT:C_W2A_BOT + P], wts[:, C_B1B:C_B1B + 1],
                                 start=True, stop=True).then_inc(wc_raw, 1)
                pe.wait_ge(wc_ready, 2)
                pe.wait_ge(flag_ready, 1)
                pe.wait_ge(p_ready, done(NTURNS))
                pe.wait_ge(ht_kept, done(NTURNS))

                def ids(slot, turn, g):
                    b = slot % 2
                    pe.wait_ge(dig_in[slot], (turn + 1) * 16)
                    pe.wait_ge(onehot_ready, done(g))
                    pe.wait_ge(same_ready, done(g - 1))
                    nc.tensor.matmul(dsts_ps[:], spread[:, 1, :], dig[:, slot, :], start=True, stop=True)
                    nc.tensor.matmul(srcs_ps[b][:], spread[:, 0, :], dig[:, slot, :], start=True, stop=True).then_inc(ids_ready, 1)

                def z(slot, turn, g):
                    b = slot % 2
                    pe.wait_ge(et_in[slot], (turn + 1) * 16)
                    pe.wait_ge(wp_in[slot], (turn + 1) * 16)
                    pe.wait_ge(relu_ready, done(g - 1))
                    pe.wait_ge(onehot_ready, done(g + 1))
                    for k in range(TPG):
                        t = nc.tensor.matmul(z_ps[b][:, k * D:(k + 1) * D], et[:, slot, k * P:(k + 1) * P], wp[:, slot, :],
                                             start=True, stop=True)
                    t.then_inc(z_ready, 1)

                def combine(slot, g):
                    b = slot % 2
                    pe.wait_ge(same_ready, done(g + 1))
                    pe.wait_ge(parts_ready, done(g + 1))
                    pe.wait_ge(rows_ready, done(g - 1))
                    for k in range(TPG):
                        nc.tensor.matmul(c_ps[b][:, k * W:(k + 1) * W], same[:, b, k, :], r_hi[:, b, k, :],
                                         start=True, stop=False)
                        nc.tensor.matmul(c_ps[b][:, k * W:k * W + D], same[:, b, k, :], r_mid[:, b, k, :],
                                         start=False, stop=False)
                        t = nc.tensor.matmul(c_ps[b][:, k * W:k * W + D], same[:, b, k, :], r_lo[:, b, k, :],
                                             start=False, stop=True)
                    t.then_inc(comb_ready, 1)

                ids(0, 0, 0)
                ids(1, 0, 1)
                z(0, 0, 0)

                def group(slot, turn, g):
                    ids((slot + 2) % RING, turn + (slot + 2) // RING, g + 2)
                    z((slot + 1) % RING, turn + (slot + 1) // RING, g + 1)
                    combine(slot, g)

                def u(i):
                    pe.wait_ge(u_ready, done(i))
                    nc.tensor.matmul(u_ps[:, 0:HALF], wts[:, C_W2A_TOP:C_W2A_TOP + P], ht[:, bass.ds(i * HALF, HALF)],
                                     start=True, stop=True).then_inc(u_raw, 1)

                main_loop(pe, group, u)
                pe.wait_ge(relu_ready, done(GROUPS + 1))
                pe.wait_ge(same_ready, done(GROUPS + 2))
                pe.wait_ge(rows_ready, done(GROUPS))

                def mean_t(b, m):
                    pe.wait_ge(a_ready, done(m + 1))
                    pe.wait_ge(at_ready, done(m - 1))
                    pe.sem_inc(pe_past, 1)
                    for j in range(PAIRS):
                        t = nc.tensor.transpose(srcs_ps[b][:, j * P:(j + 1) * P], pair(a_st, b, j), ident[:])
                    t.then_inc(at_raw, 1)

                def hidden(b, m):
                    pe.wait_ge(at_ready, done(m + 1))
                    pe.wait_ge(hsum_ready, done(m - 1))
                    nc.tensor.matmul(z_ps[b][:, 0:HALF], wcq[:, 0:P], at_st[:, b, :], start=True, stop=True).then_inc(hid_raw, 1)

                def met_t(b, m):
                    pe.wait_ge(met_ready, done(m + 1))
                    pe.wait_ge(ustar_ready, done(m - 1))
                    for j in range(PAIRS):
                        t = nc.tensor.matmul(met_ps[b][:, j * P:(j + 1) * P], pair(met, b, j), ident_b[:], start=True, stop=True)
                    t.then_inc(met_raw, 1)

                def out_rows(b, m):
                    pe.wait_ge(hid_ready, done(m + 1))
                    pe.wait_ge(res_ready, done(m - 1))
                    for j in range(PAIRS):
                        t = nc.tensor.matmul(c_ps[b][:, j * P:(j + 1) * P], hid_st[:, b, j * P:(j + 1) * P],
                                             wts[:, C_W2B:C_W2B + P], start=True, stop=True)
                    t.then_inc(res_raw, 1)

                pe.wait_ge(ident_b_ready, 1)
                pe.wait_ge(u_ready, done(NTURNS))
                pipelined(pe, [(1, hidden), (2, mean_t), (0, out_rows), (2, met_t)])


def kernel(x, src, dst, edge_attr_64, L0_gnn_u, L0_gnn_W1a, L0_gnn_b1a, L0_gnn_W1b, L0_gnn_b1b, L0_gnn_W2a, L0_gnn_b2a,
           L0_gnn_W2b, L0_gnn_b2b):
    import numpy as np
    import concourse.bacc as bacc
    from concourse.bass_utils import run_bass_kernel_spmd

    more = EDGES - N_EDGES
    e_t = np.pad(np.asarray(edge_attr_64), ((0, more), (0, 0))).T
    src_p = np.pad(np.asarray(src), (0, more), constant_values=PAD_NODE)
    dst_p = np.pad(np.asarray(dst), (0, more), mode="edge")
    w1a, w1b, w2a, w2b = (np.asarray(w) for w in (L0_gnn_W1a, L0_gnn_W1b, L0_gnn_W2a, L0_gnn_W2b))
    b1a, b1b, b2a, b2b = (np.asarray(b) for b in (L0_gnn_b1a, L0_gnn_b1b, L0_gnn_b2a, L0_gnn_b2b))

    def twice(w):
        return np.block([[w, np.zeros_like(w)], [np.zeros_like(w), w]])

    parts = [np.pad(w1a[D:], ((0, P - D), (0, 0))), twice(w1a[:D]), twice(w1b.T), twice(w2a[:D]), twice(w2a[D:]), twice(w2b),
             np.tile(b1b, 2)[:, None], np.tile(b2a, 2)[:, None]]
    arrays = {
        "x": np.pad(np.asarray(x), ((0, NODES - N_NODES), (0, 0))),
        "e_t": e_t,
        "src_col": src_p.reshape(COLS, P).T, "dst_col": dst_p.reshape(COLS, P).T,
        "src_row": src_p.reshape(ROWP, ROWG * GE), "dst_row": dst_p.reshape(ROWP, ROWG * GE),
        "weights": np.concatenate(parts, axis=1),
        "row_biases": np.concatenate([b1a, b2b])[None],
    }
    arrays = {"in_" + n: np.ascontiguousarray(a) for n, a in arrays.items()}
    nc = bacc.Bacc("TRN2", target_bir_lowering=False, num_devices=1)
    args = [nc.dram_tensor(n, a.shape, mybir.dt.from_np(a.dtype), kind="ExternalInput").ap() for n, a in arrays.items()]
    out = nc.dram_tensor("out_0", (N_NODES, D), mybir.dt.float32, kind="ExternalOutput").ap()
    gnn_kernel(nc, *args, out)
    r = run_bass_kernel_spmd(nc, [arrays], core_ids=[0])
    return r.results[0]["out_0"]
```
